# Optimizing a Trainium2 kernel written in Bass

```python
import numpy as np
import jax
import jax.numpy as jnp

def _softmax(x, axis=-1):
    return jax.nn.softmax(x, axis=axis)

def _gelu(x):
    return jax.nn.gelu(x, approximate=True)

def _silu(x):
    return jax.nn.silu(x)

def _sigmoid(x):
    return jax.nn.sigmoid(x)

def _layernorm(x, axis=-1, eps=1e-05):
    m = jnp.mean(x, axis=axis, keepdims=True)
    v = jnp.var(x, axis=axis, keepdims=True)
    return (x - m) / jnp.sqrt(v + eps)

def _scatter_add(tgt, idx, src, axis=0):
    return tgt.at[idx].add(src)

def _segment_sum(src, seg, n):
    return jax.ops.segment_sum(src, seg, n)
kernel_name = 'mk_seq_preln_d1_jaxref_r4_85541d'

def setup_inputs(seed: int=0):
    np.random.seed(seed)
    _w = jnp.asarray

    def _L0_attn_setup():
        import jax, jax.numpy as jnp
        import numpy as np
        B, T, D, H = (64, 128, 256, 256)
        key = jax.random.key(seed)
        k1, k2, k3 = jax.random.split(key, 3)
        scale = 0.02
        return {'x': jax.random.normal(k1, (B, T, D), dtype=jnp.float32), 'Wi': jax.random.normal(k2, (H, D), dtype=jnp.float32) * scale, 'bi': jnp.zeros((H,), dtype=jnp.float32), 'Wh': jax.random.normal(k3, (H, H), dtype=jnp.float32) * scale, 'bh': jnp.zeros((H,), dtype=jnp.float32)}
    _L0_attn_in = _L0_attn_setup()

    def _L0_ffn_setup():
        import jax, jax.numpy as jnp
        import numpy as np
        B, T, D = (4, 512, 256)
        H, DH, E, SEL = (8, 64, 5, 2)

        def _topk_mask(logits, k):
            _, idx = jax.lax.top_k(logits, k)
            return jnp.sum(jax.nn.one_hot(idx, logits.shape[-1], dtype=logits.dtype), axis=-2)
        key = jax.random.key(seed)
        ks = jax.random.split(key, 7)
        s = 0.02
        x = jax.random.normal(ks[0], (B, T, D), dtype=jnp.float32)
        Wq = jax.random.normal(ks[1], (D, H * DH), dtype=jnp.float32) * s
        Wk = jax.random.normal(ks[2], (D, H * DH), dtype=jnp.float32) * s
        Ws = jax.random.normal(ks[3], (D, H * E), dtype=jnp.float32) * s
        Wd = jax.random.normal(ks[4], (D, H * E), dtype=jnp.float32) * s
        Wv = jax.random.normal(ks[5], (E, D, DH), dtype=jnp.float32) * s
        Wo = jax.random.normal(ks[6], (E, DH, D), dtype=jnp.float32) * s
        return {'x': x, 'Wq': Wq, 'Wk': Wk, 'Ws': Ws, 'Wd': Wd, 'Wv': Wv, 'Wo': Wo}
    _L0_ffn_in = _L0_ffn_setup()
    _d = {'L0_attn_x': _L0_attn_in['x'], 'L0_attn_Wi': _L0_attn_in['Wi'], 'L0_attn_bi': _L0_attn_in['bi'], 'L0_attn_Wh': _L0_attn_in['Wh'], 'L0_attn_bh': _L0_attn_in['bh'], 'L0_ffn_Wq': _L0_ffn_in['Wq'], 'L0_ffn_Wk': _L0_ffn_in['Wk'], 'L0_ffn_Ws': _L0_ffn_in['Ws'], 'L0_ffn_Wd': _L0_ffn_in['Wd'], 'L0_ffn_Wv': _L0_ffn_in['Wv'], 'L0_ffn_Wo': _L0_ffn_in['Wo']}
    _x0 = _d['L0_attn_x']
    _d['L0_attn_x'] = jax.random.normal(jax.random.fold_in(jax.random.key(seed), 1), (2, 2048, 256), dtype=_x0.dtype)
    del _x0
    return _d

def reference(L0_attn_x, L0_attn_Wi, L0_attn_bi, L0_attn_Wh, L0_attn_bh, L0_ffn_Wq, L0_ffn_Wk, L0_ffn_Ws, L0_ffn_Wd, L0_ffn_Wv, L0_ffn_Wo):

    def _L0_attn_ref(x, Wi, bi, Wh, bh):
        import jax, jax.numpy as jnp
        import numpy as np
        B, T, D, H = (64, 128, 256, 256)
        xi = jnp.einsum('btd,hd->bth', x, Wi) + bi

        def step(h, xt):
            h_new = jnp.tanh(xt + h @ Wh.T + bh)
            return (h_new, h_new)
        h0 = jnp.zeros((x.shape[0], Wh.shape[0]), dtype=x.dtype)
        _, hs = jax.lax.scan(step, h0, jnp.swapaxes(xi, 0, 1))
        return jnp.swapaxes(hs, 0, 1)

    def _L0_ffn_ref(x, Wq, Wk, Ws, Wd, Wv, Wo):
        import jax, jax.numpy as jnp
        import numpy as np
        B, T, D = (4, 512, 256)
        H, DH, E, SEL = (8, 64, 5, 2)

        def _topk_mask(logits, k):
            _, idx = jax.lax.top_k(logits, k)
            return jnp.sum(jax.nn.one_hot(idx, logits.shape[-1], dtype=logits.dtype), axis=-2)
        e, d, dh = Wv.shape
        h = Wq.shape[1] // dh
        b, t, _ = x.shape
        scale = dh ** (-0.5)
        q = (x @ Wq).reshape(b, t, h, dh).transpose(0, 2, 1, 3)
        k = (x @ Wk).reshape(b, t, h, dh).transpose(0, 2, 1, 3)
        gl_v = (x @ Ws).reshape(b, t, h, e)
        wv = _topk_mask(gl_v, SEL) * jax.nn.sigmoid(gl_v)
        xv = jnp.einsum('btd,edk->btek', x, Wv)
        v = jnp.einsum('bthe,btek->bhtk', wv, xv)
        scores = jnp.einsum('bhid,bhjd->bhij', q * scale, k)
        probs = jax.nn.softmax(scores, axis=-1)
        attn = jnp.einsum('bhij,bhjd->bihd', probs, v)
        gl_o = (x @ Wd).reshape(b, t, h, e)
        mask_o = _topk_mask(gl_o, SEL)
        out = jnp.einsum('bthe,bthk,ekd->btd', mask_o, attn, Wo)
        return out
    x = L0_attn_x
    x = x + _L0_attn_ref(_layernorm(x, axis=-1), L0_attn_Wi, L0_attn_bi, L0_attn_Wh, L0_attn_bh)
    x = x + _L0_ffn_ref(_layernorm(x, axis=-1), L0_ffn_Wq, L0_ffn_Wk, L0_ffn_Ws, L0_ffn_Wd, L0_ffn_Wv, L0_ffn_Wo)
    return x

_drawn_inputs = setup_inputs


def setup_inputs(seed=0):
    import zlib

    import numpy as np

    out = dict(_drawn_inputs(seed))
    spreads = {'L0_attn_bi': (0.0, 0.1), 'L0_attn_bh': (0.0, 0.1)}
    factors = {'L0_ffn_Wq': 8.0,
     'L0_ffn_Wk': 8.0,
     'L0_ffn_Ws': 7.448,
     'L0_ffn_Wd': 5.795,
     'L0_ffn_Wv': 2.752,
     'L0_ffn_Wo': 2.773}
    for name, (base, spread) in spreads.items():
        noise = np.random.default_rng([zlib.crc32(name.encode()), seed]).standard_normal(out[name].shape)
        drawn = base * np.exp(spread * noise) if base else spread * noise
        out[name] = jnp.asarray(drawn.astype(out[name].dtype))
    for name, factor in factors.items():
        out[name] = (out[name] * factor).astype(out[name].dtype)
    return out
```

```python
from contextlib import ExitStack

import concourse.bass as bass
from concourse import mybir

F32 = mybir.dt.float32
F32R = mybir.dt.float32r
I32 = mybir.dt.int32
ALU = mybir.AluOpType
ACT = mybir.ActivationFunctionType
AX = mybir.AxisListType
RMAX = bass.bass_isa.ReduceOp.max

P = 128
B, T, D = 2, 2048, 256
DC = D // P
H, DH, E, SEL = 8, 64, 5, 2
EPS = 1e-5

C = P // B
L = T // C
WARM = 16
TOLERANCE = 2.0 ** -21

JT = T // P
XV = E * DH
GL = 2 * H * E
PAIRS = H // 2


def build(nc, x, wi_t, wh_t, bi, bh, wq, wk, w_tok, wo, out):
    dram = {
        name: nc.dram_tensor(name, shape, F32, kind="Internal").ap()
        for name, shape in (
            ("x1_dram", [B, T, D]),
            ("x2t_dram", [P, DC, B, T]),
            ("xv_dram", [B, JT, P, XV]),
        )
    }
    with ExitStack() as ctx:
        ident = ctx.enter_context(nc.sbuf_tensor("ident", [P, P], F32))
        gates = ctx.enter_context(nc.sbuf_tensor("gates", [P, B * JT, 2 * H, E], F32))
        prepare(nc, dram, x, wi_t, wh_t, bi, bh, w_tok, ident, gates)
        attend(nc, dram, wq, wk, wo, ident, gates, out)


def rsqrt(v, link, y, var, tmp, tmp_bits, var_bits, y_bits):
    link(v.tensor_scalar(tmp_bits, var_bits, 1, None, ALU.logical_shift_right))
    link(v.tensor_scalar(y_bits, tmp_bits, -1.0, float(0x5F3759DF), ALU.mult, ALU.add))
    for _ in range(4):
        link(v.tensor_tensor(tmp, y, y, ALU.mult))
        link(v.tensor_tensor(tmp, tmp, var, ALU.mult))
        link(v.tensor_scalar(tmp, tmp, -0.5, 1.5, ALU.mult, ALU.add))
        link(v.tensor_tensor(y, y, tmp, ALU.mult))


def prepare(nc, dram, x, wi_t, wh_t, bi, bh, w_tok, ident, gates):
    with ExitStack() as ctx:
        def sb(name, shape, dt=F32):
            return ctx.enter_context(nc.sbuf_tensor(name, shape, dt))

        def psum(name):
            return ctx.enter_context(nc.psum_tensor(name, [P, 512], F32))

        def sem(name):
            return ctx.enter_context(nc.semaphore(name))

        x_sb = sb("x_sb", [P, L, D])
        xn = sb("xn", [P, L, D])
        xn_t = sb("xn_t", [P, DC, L, P])
        x2_t = xn_t[:].rearrange("p k s n -> p k (s n)").rearrange("p k (b n) -> p k b n", b=B)
        h_t = sb("h_t", [P, DC, L + 1, P])
        wi_sb = sb("wi_sb", [P, DC, D])
        wh_sb = sb("wh_sb", [P, DC, D])
        w_tok_sb = sb("w_tok_sb", [P, DC, XV + GL])
        bias2 = sb("bias2", [P, 2, DC])
        bias = sb("bias", [P, DC])
        st = sb("st", [P, L, 6])
        sm = sb("sm", [P, 7, L])
        mean, rstd, var = sm[:, 0, :], sm[:, 1, :], sm[:, 2, :]
        diff = sb("diff", [P, DC, B, C - 1])
        worst = sb("worst", [P, 2])
        flag = sb("flag", [P, 1], I32)
        tok_sb = sb("tok_sb", [P, 2, XV + GL])
        logit = sb("logit", [P, B * JT, 2 * H, E])
        rank = sb("rank", [P, B * JT, 2 * H, E])
        above = sb("above", [P, B * JT, 2 * H, E - 1])
        z = [[psum(f"z{p}{m}") for m in range(DC)] for p in range(2)]
        tp = [psum(f"tp{p}") for p in range(2)]
        tk = [psum(f"tk{p}") for p in range(2)]

        x_in = [sem(f"x_in{g}") for g in range(4)]
        w_in, w_tok_in = sem("w_in"), sem("w_tok_in")
        ident_zero, ident_ok = sem("ident_zero"), sem("ident_ok")
        dve = sem("dve_chain")
        norm1, tp1, tp1_act, tp1_dve = sem("norm1"), sem("tp1"), sem("tp1_act"), sem("tp1_dve")
        bias_ok = sem("bias_ok")
        z_ready, h_ready = sem("z_ready"), sem("h_ready")
        started, mismatch, reduced, flagged = sem("started"), sem("mismatch"), sem("reduced"), sem("flagged")
        back, added, norm2 = sem("back"), sem("added"), sem("norm2")
        tp2, tp2_out = sem("tp2"), sem("tp2_out")
        tok, tok_out, logits_out = sem("tok"), sem("tok_out"), sem("logits_out")
        xv_stored, stored = [sem("xv_stored0"), sem("xv_stored1")], sem("stored")
        ranks_zero, compared, exp_done = sem("ranks_zero"), sem("compared"), sem("exp_done")

        x_rows = x.rearrange("b (c s) d -> (b c) s d", s=L)
        G = L // 4
        GROUPS = [2, 3, 0, 1]
        PAIR_ORDER = [j for g in GROUPS for j in range(g * G // 2, (g + 1) * G // 2)]
        count = [0]

        def logit_of(t):
            return logit[:, (t % B) * JT + t // B].rearrange("p g e -> p (g e)")

        def link(ins):
            count[0] += 1
            ins.then_inc(dve, 1)
            nc.vector.wait_ge(dve, count[0])

        def statistics(lo, n):
            s = slice(lo, lo + n)
            v = nc.vector
            a, b2 = sm[:, 3, s], sm[:, 4, s]
            link(v.tensor_tensor(a, st[:, s, 1], st[:, s, 4], ALU.subtract))
            link(v.tensor_tensor(mean[:, s], st[:, s, 1], st[:, s, 4], ALU.add))
            link(v.tensor_tensor(b2, st[:, s, 2], st[:, s, 5], ALU.add))
            link(v.tensor_tensor(a, a, a, ALU.mult))
            link(v.tensor_scalar(mean[:, s], mean[:, s], 0.5, None, ALU.mult))
            link(v.tensor_scalar(b2, b2, 1.0 / D, EPS, ALU.mult, ALU.add))
            link(v.scalar_tensor_tensor(var[:, s], a, 0.25, b2, ALU.mult, ALU.add))
            rsqrt(v, link, rstd[:, s], var[:, s], a, a.bitcast(I32), var[:, s].bitcast(I32),
                  rstd[:, s].bitcast(I32))

        with nc.Block() as block:

            @block.sync
            def _(sp):
                for n, g in enumerate(GROUPS):
                    sp.dma_start(x_sb[:, g * G:(g + 1) * G, :], x_rows[:, g * G:(g + 1) * G, :]
                                 ).then_inc(x_in[n], 16)
                    if n == 0:
                        sp.dma_start(wi_sb[:], wi_t.rearrange("(k p) h -> p k h", p=P)).then_inc(w_in, 16)
                        sp.dma_start(wh_sb[:], wh_t.rearrange("(k p) h -> p k h", p=P)).then_inc(w_in, 16)
                        sp.dma_start(bias2[:, 0, :], bi).then_inc(w_in, 16)
                        sp.dma_start(bias2[:, 1, :], bh).then_inc(w_in, 16)
                sp.dma_start(w_tok_sb[:], w_tok.rearrange("(k p) n -> p k n", p=P)).then_inc(w_tok_in, 16)
                for t in range(B * JT):
                    sp.wait_ge(tok_out, t + 1)
                    sp.dma_start(dram["xv_dram"][t % B, t // B], tok_sb[:, t % 2, 0:XV]
                                 ).then_inc(xv_stored[t % 2], 16)
                sp.wait_ge(added, L)
                for b in range(B):
                    sp.dma_start(dram["x1_dram"][b].rearrange("(s c) d -> c s d", c=C),
                                 x_sb[b * C:(b + 1) * C, :, :]).then_inc(stored, 16)
                sp.dma_start(dram["x2t_dram"], x2_t).then_inc(stored, 16)
                sp.wait_ge(stored, 16 * (B + 1))
                for p in range(2):
                    sp.wait_ge(xv_stored[p], 16 * B * JT // 2)

            @block.gpsimd
            def _(pool):
                nc.gpsimd.memset(ident[:], 0.0).then_inc(ident_zero, 1)
                pool.wait_ge(ident_zero, 1)
                nc.gpsimd.affine_select(out=ident[:], in_=ident[:], compare_op=ALU.not_equal, fill=1.0,
                                        base=0, pattern=[[-1, P]], channel_multiplier=1).then_inc(ident_ok, 1)
                pool.wait_ge(mismatch, 1)
                nc.gpsimd.partition_all_reduce(worst[:, 1:2], worst[:, 0:1], P, RMAX).then_inc(reduced, 1)
                for e in range(E):
                    nc.gpsimd.memset(rank[:, :, :, e], float(e)).then_inc(ranks_zero, 1)
                for t in range(B * JT):
                    pool.wait_ge(tok_out, t + 1)
                    nc.gpsimd.tensor_copy(logit_of(t), tok_sb[:, t % 2, XV:XV + GL]
                                          ).then_inc(logits_out, 1)

            @block.vector
            def _(dve_eng):
                v = nc.vector
                link(v.memset(h_t[:, :, 0, :], 0.0))

                def normalise1(half):
                    for n in (2 * half, 2 * half + 1):
                        g = GROUPS[n]
                        dve_eng.wait_ge(x_in[n], 16)
                        for s in range(g * G, (g + 1) * G):
                            link(v.bn_stats(st[:, s, :], x_sb[:, s, :]))
                    lo = GROUPS[2 * half] * G
                    statistics(lo, 2 * G)
                    for s in range(lo, lo + 2 * G):
                        v.tensor_scalar(xn[:, s, :], x_sb[:, s, :], mean[:, s:s + 1], rstd[:, s:s + 1],
                                        ALU.subtract, ALU.mult).then_inc(norm1, 1)

                normalise1(0)
                dve_eng.wait_ge(w_in, 64)
                v.tensor_tensor(bias[:], bias2[:, 0, :], bias2[:, 1, :], ALU.add).then_inc(bias_ok, 1)
                normalise1(1)
                for n in range(L // 4, L // 2):
                    dve_eng.wait_ge(tp1, n + 1)
                    v.tensor_copy(xn_t[:, :, 2 * PAIR_ORDER[n]:2 * PAIR_ORDER[n] + 2, :],
                                  tp[n % 2][:].rearrange("p (k s n) -> p k s n", k=DC, s=2)
                                  ).then_inc(tp1_dve, 1)

                def start_states(steps):
                    dve_eng.wait_ge(h_ready, 2 * steps)
                    for k in range(DC):
                        last = v.tensor_copy(
                            h_t[:, k, 0, :].rearrange("p (b c) -> p b c", b=B)[:, :, 1:C],
                            h_t[:, k, L, :].rearrange("p (b c) -> p b c", b=B)[:, :, 0:C - 1])
                        last.then_inc(started, 1)

                start_states(WARM)
                dve_eng.wait_ge(h_ready, 2 * (WARM + L))
                for k in range(DC):
                    link(v.tensor_tensor(diff[:, k],
                                         h_t[:, k, L, :].rearrange("p (b c) -> p b c", b=B)[:, :, 0:C - 1],
                                         h_t[:, k, 0, :].rearrange("p (b c) -> p b c", b=B)[:, :, 1:C],
                                         ALU.subtract))
                v.tensor_reduce(worst[:, 0:1], diff[:].rearrange("p k b c -> p (k b c)"), AX.X, ALU.max,
                                apply_absolute_value=True).then_inc(mismatch, 1)
                dve_eng.wait_ge(reduced, 1)
                v.tensor_scalar(flag[:], worst[:, 1:2], TOLERANCE, None, ALU.is_gt).then_inc(flagged, 1)
                dve_eng.wait_ge(flagged, 1)
                again = v.value_load(flag[0:1, 0:1], min_val=0, max_val=1)
                with dve_eng.If(again == 1):
                    with dve_eng.Fori(0, C - 1) as r:
                        start_states(r * L + (WARM + L))
                    dve_eng.wait_ge(h_ready, 2 * (WARM + C * L))

                for g in range(4):
                    for s in range(g * G, (g + 1) * G):
                        dve_eng.wait_ge(back, s + 1)
                        v.tensor_tensor(x_sb[:, s, :], tp[s % 2][:, 0:D], x_sb[:, s, :], ALU.add
                                        ).then_inc(added, 1)
                        dve_eng.wait_ge(added, s + 1)
                        link(v.bn_stats(st[:, s, :], x_sb[:, s, :]))
                    statistics(g * G, G)
                    for s in range(g * G, (g + 1) * G):
                        v.tensor_scalar(xn[:, s, :], x_sb[:, s, :], mean[:, s:s + 1], rstd[:, s:s + 1],
                                        ALU.subtract, ALU.mult).then_inc(norm2, 1)

                dve_eng.wait_ge(ranks_zero, E)
                dve_eng.wait_ge(logits_out, B * JT)
                for d in range(1, E):
                    gt = above[:, :, :, 0:E - d]
                    link(v.tensor_tensor(gt, logit[:, :, :, d:E], logit[:, :, :, 0:E - d], ALU.is_gt))
                    link(v.tensor_tensor(rank[:, :, :, 0:E - d], rank[:, :, :, 0:E - d], gt, ALU.add))
                    link(v.tensor_tensor(rank[:, :, :, d:E], rank[:, :, :, d:E], gt, ALU.subtract))
                v.tensor_scalar(rank[:], rank[:], SEL - 0.5, None, ALU.is_lt).then_inc(compared, 1)
                dve_eng.wait_ge(compared, 1)
                v.tensor_copy(gates[:, :, H:2 * H, :], rank[:, :, H:2 * H, :])
                sig = logit[:, :, 0:H, :]
                dve_eng.wait_ge(exp_done, 1)
                link(v.tensor_scalar(sig, sig, 1.0, None, ALU.add))
                link(v.reciprocal(sig, sig))
                link(v.tensor_tensor(gates[:, :, 0:H, :], rank[:, :, 0:H, :], sig, ALU.mult))

            @block.tensor
            def _(pe):
                def transpose_pair(n, j, normed, done):
                    for s2 in range(2):
                        for k in range(DC):
                            last = nc.tensor.transpose(
                                normed[n % 2][:, (2 * k + s2) * P:(2 * k + s2 + 1) * P],
                                xn[:, 2 * j + s2, k * P:(k + 1) * P], ident[:])
                    last.then_inc(done, 1)

                def transposes1(lo, hi):
                    for n in range(lo, hi):
                        pe.wait_ge(norm1, 2 * n + 2)
                        if n >= 2 and n - 1 <= L // 4:
                            pe.wait_ge(tp1_act, n - 1)
                        elif n >= 2:
                            pe.wait_ge(tp1_dve, n - 1 - L // 4)
                        transpose_pair(n, PAIR_ORDER[n], tp, tp1)

                def x_part(q, s, alone=False):
                    for m in range(DC):
                        for k in range(DC):
                            last = nc.tensor.matmul(z[q % 2][m][:, 0:P], wi_sb[:, k, m * P:(m + 1) * P],
                                                    xn_t[:, k, s, :], start=(k == 0),
                                                    stop=alone and k == DC - 1)
                        if alone:
                            last.then_inc(z_ready, 1)

                def h_part(parity, steps, slot):
                    for k in range(DC):
                        pe.wait_ge(h_ready, steps * 2 - 1 + k)
                        for m in range(DC):
                            last = nc.tensor.matmul(z[parity][m][:, 0:P], wh_sb[:, k, m * P:(m + 1) * P],
                                                    h_t[:, k, slot, :], start=False, stop=(k == DC - 1))
                            if k == DC - 1:
                                last.then_inc(z_ready, 1)

                def sweep(steps):
                    with pe.Fori(0, L // 2 - 1) as i:
                        h_part(0, i * 2 + steps, i * 2)
                        x_part(1, i * 2 + 1)
                        h_part(1, i * 2 + (steps + 1), i * 2 + 1)
                        x_part(0, i * 2 + 2)
                    h_part(0, steps + (L - 2), L - 2)
                    x_part(1, L - 1)
                    h_part(1, steps + (L - 1), L - 1)

                pe.wait_ge(ident_ok, 1)
                transposes1(0, L // 4)
                pe.wait_ge(w_in, 64)
                pe.wait_ge(tp1_act, L // 4)
                x_part(0, L - WARM, alone=True)
                x_part(1, L - WARM + 1)
                with pe.Fori(0, WARM // 2 - 1) as i:
                    h_part(1, i * 2 + 1, i * 2 + (L - WARM + 1))
                    x_part(0, i * 2 + (L - WARM + 2))
                    h_part(0, i * 2 + 2, i * 2 + (L - WARM + 2))
                    x_part(1, i * 2 + (L - WARM + 3))
                h_part(1, WARM - 1, L - 1)
                transposes1(L // 4, L // 2)
                pe.wait_ge(tp1_dve, L // 4)
                x_part(0, 0)
                pe.wait_ge(started, DC)
                sweep(WARM)
                pe.wait_ge(flagged, 1)
                again = nc.tensor.value_load(flag[0:1, 0:1], min_val=0, max_val=1)
                with pe.If(again == 1):
                    with pe.Fori(0, C - 1) as r:
                        x_part(0, 0)
                        pe.wait_ge(started, r * DC + 2 * DC)
                        for s in range(L):
                            h_part(s % 2, r * L + (WARM + L + s), s)
                            if s < L - 1:
                                x_part((s + 1) % 2, s + 1)
                    pe.wait_ge(h_ready, 2 * (WARM + C * L))
                pe.wait_ge(w_tok_in, 16)

                def back_to_rows(s):
                    if s >= 2:
                        pe.wait_ge(added, s - 1)
                    for k in range(DC):
                        last = nc.tensor.transpose(tp[s % 2][:, k * P:(k + 1) * P], h_t[:, k, s + 1, :],
                                                   ident[:])
                    last.then_inc(back, 1)

                pe.wait_ge(h_ready, 2 * (WARM + L))
                for g in range(5):
                    if g < 4:
                        for s in range(g * G, (g + 1) * G):
                            back_to_rows(s)
                    if g > 0:
                        for j in range((g - 1) * G // 2, g * G // 2):
                            pe.wait_ge(norm2, 2 * j + 2)
                            if j >= 2:
                                pe.wait_ge(tp2_out, 2 * (j - 1))
                            transpose_pair(j, j, tk, tp2)
                            pe.wait_ge(tp2_out, 2 * (j + 1))
                            for b in range(B):
                                t = 2 * j + b
                                if t >= 2:
                                    pe.wait_ge(tok_out, t - 1)
                                for k in range(DC):
                                    last = nc.tensor.matmul(z[0][b][:, 0:XV + GL],
                                                            x2_t[:, k, b, j * P:(j + 1) * P],
                                                            w_tok_sb[:, k, :], start=(k == 0),
                                                            stop=(k == DC - 1))
                                last.then_inc(tok, 1)

            @block.scalar
            def _(act):
                for n in range(L // 4):
                    act.wait_ge(tp1, n + 1)
                    nc.scalar.activation(xn_t[:, :, 2 * PAIR_ORDER[n]:2 * PAIR_ORDER[n] + 2, :],
                                         tp[n % 2][:].rearrange("p (k s n) -> p k s n", k=DC, s=2),
                                         ACT.Copy).then_inc(tp1_act, 1)
                act.wait_ge(bias_ok, 1)

                def step(parity, steps, slot):
                    for m in range(DC):
                        act.wait_ge(z_ready, steps * 2 + m + 1)
                        nc.scalar.activation(h_t[:, m, slot, :], z[parity][m][:, 0:P], ACT.Tanh,
                                             bias=bias[:, m:m + 1]).then_inc(h_ready, 1)

                with act.Fori(0, WARM // 2) as i:
                    step(0, i * 2, i * 2 + (L - WARM + 1))
                    step(1, i * 2 + 1, i * 2 + (L - WARM + 2))
                with act.Fori(0, L // 2) as i:
                    step(0, i * 2 + WARM, i * 2 + 1)
                    step(1, i * 2 + (WARM + 1), i * 2 + 2)
                act.wait_ge(flagged, 1)
                again = nc.scalar.value_load(flag[0:1, 0:1], min_val=0, max_val=1)
                with act.If(again == 1):
                    with act.Fori(0, C - 1) as r:
                        for s in range(L):
                            step(s % 2, r * L + (WARM + L + s), s + 1)
                for j in range(L // 2):
                    act.wait_ge(tp2, j + 1)
                    for k in range(DC):
                        nc.scalar.activation(
                            x2_t[:, k, :, j * P:(j + 1) * P].rearrange("p b (s c) -> p b s c", s=2),
                            tk[j % 2][:, 2 * k * P:2 * (k + 1) * P].rearrange("p (s b c) -> p b s c", s=2, b=B),
                            ACT.Copy).then_inc(tp2_out, 1)
                    for b in range(B):
                        t = 2 * j + b
                        act.wait_ge(tok, t + 1)
                        if t >= 2:
                            act.wait_ge(logits_out, t - 1)
                            act.wait_ge(xv_stored[t % 2], 16 * (t // 2))
                        nc.scalar.activation(tok_sb[:, t % 2, :], z[0][b][:, 0:XV + GL], ACT.Copy
                                             ).then_inc(tok_out, 1)
                act.wait_ge(compared, 1)
                nc.scalar.activation(logit[:, :, 0:H, :], logit[:, :, 0:H, :], ACT.Exp, scale=-1.0
                                     ).then_inc(exp_done, 1)


SCALE = DH ** -0.5
CH = 512
NCH = T // CH
ROWS = 2 * JT
UNITS = JT // 2
PBUF = 3
LAG_T = 2
LAG_AV = 6
SLOTS = ROWS + LAG_AV
AV_STEPS = JT // 4


def transposes_in(slot):
    return slot - LAG_T if LAG_T <= slot < ROWS + LAG_T else None


def product_in(slot):
    n = slot - LAG_AV
    return (n // 4, n % 4) if n >= 0 and n // 4 < UNITS else (None, None)


def projections_in(slot):
    return [n for n in range(2 * NCH) if slot == PROJ_SLOT[n]]


PROJ_SLOT = [32, 32, 33, 33, 34, 35, 36, 37]


def output_in(slot):
    n = slot - LAG_AV - 4
    return n // 4 if n >= 0 and n % 4 == 0 and n // 4 < UNITS else None


def ring_numbers():
    use, by_act, by_dve = {}, {}, {}

    def add(key, act, dve):
        use[key] = len(use)
        if act:
            by_act[key] = len(by_act)
        if dve:
            by_dve[key] = len(by_dve)

    for slot in range(SLOTS + 1):
        if transposes_in(slot) is not None:
            for g in range(4):
                add(("t", transposes_in(slot), g), g != 1, g == 1)
        for n in projections_in(slot):
            add(("p", n), True, True)
        if output_in(slot) is not None:
            add(("o", output_in(slot)), False, True)
    return use, by_act, by_dve


def attend(nc, dram, wq, wk, wo, ident, gates, out):
    USE, ACT_NO, DVE_NO = ring_numbers()
    N_USE, N_ACT, N_DVE = len(USE), len(ACT_NO), len(DVE_NO)
    FIRST = 2 * NCH
    with ExitStack() as ctx:
        def sb(name, shape, dt=F32):
            return ctx.enter_context(nc.sbuf_tensor(name, shape, dt))

        def psum(name, n):
            return ctx.enter_context(nc.psum_tensor(name, [P, n], F32))

        def sem(name):
            return ctx.enter_context(nc.semaphore(name))

        xc = sb("xc", [P, 2, DC, CH])
        w_pair = sb("w_pair", [P, DC, 2, P])
        q_s = sb("q_s", [P, 2, T], F32R)
        k_hi = sb("k_hi", [P, 2, T], F32R)
        k_lo = sb("k_lo", [P, 2, T], F32R)
        q_low = sb("q_low", [P, 2, CH], F32R)
        probs = sb("probs", [P, PBUF, T])
        probs_t = sb("probs_t", [P, 2, JT, 2, 2 * P])
        least = sb("least", [P, ROWS, 2])
        sums = sb("sums", [P, ROWS, 2])
        inv = sb("inv", [P, 4])
        v_sb = sb("v_sb", [P, JT, 2, DH])
        v_next = sb("v_next", [P, JT, 2, DH])
        xv_c = sb("xv_c", [P, 2, 2, E, DH])
        gate_v = sb("gate_v", [P, JT, 2, E])
        gate_o = sb("gate_o", [P, JT, 2, E])
        mixed = sb("mixed", [P, 2, E, DH])
        o_t = sb("o_t", [P, 2, 2 * P])
        o_rows = sb("o_rows", [P, 2, 2, 2, DH])
        acc = sb("acc", [P, JT, E, DH])
        wo_sb = sb("wo_sb", [P, 3, D])
        s_ps = [psum(f"s_ps{c}", 2 * CH) for c in range(2)]
        ring = [psum(f"ring{p}", CH) for p in range(2)]
        av = [psum(f"av{p}", CH) for p in range(2)]
        acc_t = probs[:, 0, 0:2 * 3 * P].rearrange("p (a c n) -> p a c n", a=2, c=3)
        last = probs[:, 1:3, :].rearrange("p a (j d) -> p (a j) d", d=D)

        x_in, w_in, wo_in = [sem("x_in_0"), sem("x_in_1")], sem("w_pair_in"), sem("wo_in")
        used, act_out, dve_out = sem("used"), sem("act_out"), sem("dve_out")
        k_in, q_in = [sem(f"k_in{c}") for c in range(NCH)], [sem(f"q_in{c}") for c in range(NCH)]
        scored, s_out, exp_out = sem("scored"), sem("s_out"), sem("exp_out")
        av_done, av_out = sem("av_done"), sem("av_out")
        xv_in, v_mixed, v_in = [sem("xv_in0"), sem("xv_in1")], sem("v_mixed"), sem("v_in")
        dve, pool_chain = sem("dve_chain2"), sem("pool_chain")
        gated, acc_zero = sem("gated"), sem("acc_zero")
        x1_in, projected, finished, out_in = sem("x1_in"), sem("projected"), sem("finished"), sem("out_in")

        def counts(eng, b, hp):
            p = b * (H // 2) + hp

            def wait(semaphore, n, per_pair, per_seq=0, before=0):
                v = p * per_pair + (n + before)
                if per_seq:
                    v = v + b * per_seq
                eng.wait_ge(semaphore, v)
            return wait

        def used_by(wait, key):
            wait(used, USE[key] + 1, N_USE, JT, FIRST)

        def act_copied(wait, key):
            wait(act_out, ACT_NO[key] + 1, N_ACT, JT, FIRST)

        def dve_copied(wait, key):
            wait(dve_out, DVE_NO[key] + 1, N_DVE, 0, FIRST)

        def copied(wait, key):
            dve_copied(wait, key) if key in DVE_NO else act_copied(wait, key)

        NUMBER = {n: key for key, n in USE.items()}

        with nc.Block() as block:

            @block.sync
            def _(sp):
                def load_weights(head_pair):
                    for n, w in enumerate((wk, wq)):
                        sp.dma_start(w_pair[:, :, n, :],
                                     w.rearrange("(k p) n -> p k n", p=P)[:, :, bass.ds(head_pair * P, P)]
                                     ).then_inc(w_in, 16)

                def load_chunk(seq, c):
                    sp.dma_start(xc[:, c % 2], dram["x2t_dram"][:, :, bass.ds(seq, 1), c * CH:(c + 1) * CH]
                                 .rearrange("p k o n -> p k (o n)")).then_inc(x_in[c % 2], 16)

                def load_values(seq, n):
                    sp.dma_start(xv_c[:, n % 2],
                                 dram["xv_dram"][bass.ds(seq, 1), 2 * n:2 * n + 2]
                                 .rearrange("o j p (e k) -> p (o j) e k", e=E)).then_inc(xv_in[n % 2], 16)

                def other_halves(c, is_query):
                    cs = slice(c * CH, (c + 1) * CH)
                    up, down = slice(0, DH), slice(DH, P)
                    if is_query:
                        sp.dma_start(q_s[down, 0, cs].bitcast(F32), q_low[up, c % 2, :].bitcast(F32)).then_inc(q_in[c], 16)
                        sp.dma_start(q_s[up, 1, cs].bitcast(F32), q_low[down, c % 2, :].bitcast(F32)).then_inc(q_in[c], 16)
                    else:
                        for k in (k_hi, k_lo):
                            sp.dma_start(k[down, 0, cs].bitcast(F32), k[up, 0, cs].bitcast(F32)).then_inc(k_in[c], 16)
                            sp.dma_start(k[up, 1, cs].bitcast(F32), k[down, 1, cs].bitcast(F32)).then_inc(k_in[c], 16)

                load_weights(0)
                for c in range(2):
                    load_chunk(0, c)
                for n in range(2):
                    load_values(0, n)
                sp.dma_start(wo_sb[:, 0:2, :], wo[0:2 * P].rearrange("(c p) d -> p c d", p=P)).then_inc(wo_in, 16)
                sp.dma_start(wo_sb[0:DH, 2, :], wo[2 * P:XV]).then_inc(wo_in, 16)
                for c in range(NCH):
                    sp.wait_ge(dve_out, 2 * c + 1)
                    other_halves(c, False)
                    sp.wait_ge(dve_out, 2 * c + 2)
                    other_halves(c, True)
                    if c < NCH - 2:
                        load_chunk(0, c + 2)
                for n in range(2, UNITS):
                    sp.wait_ge(v_mixed, n - 1)
                    load_values(0, n)
                sp.wait_ge(v_mixed, UNITS)
                sp.dma_start(v_sb[:], v_next[:]).then_inc(v_in, 16)

                with sp.Fori(0, B) as b:
                    with sp.Fori(0, PAIRS) as hp:
                        wait = counts(sp, b, hp)
                        following = (b * PAIRS + hp + 1) % (B * PAIRS)
                        seq, pair = sp.snap(following // PAIRS), sp.snap(following % PAIRS)
                        for n in range(UNITS):
                            wait(v_mixed, n - 1, UNITS, 0, UNITS)
                            load_values(seq, n)
                        load_weights(pair)
                        for c in range(2):
                            load_chunk(seq, c)
                        for c in range(NCH):
                            dve_copied(wait, ("p", 2 * c))
                            other_halves(c, False)
                            dve_copied(wait, ("p", 2 * c + 1))
                            other_halves(c, True)
                            if c < NCH - 2:
                                load_chunk(seq, c + 2)
                        wait(v_mixed, UNITS, UNITS, 0, UNITS)
                        wait(av_done, UNITS, UNITS)
                        sp.dma_start(v_sb[:], v_next[:]).then_inc(v_in, 16)
                    sp.wait_ge(used, b * (PAIRS * N_USE + JT) + (FIRST + PAIRS * N_USE))
                    for n in range(2):
                        sp.dma_start(last[:, 8 * n:8 * n + 8, :],
                                     dram["x1_dram"][bass.ds(b, 1), n * T // 2:(n + 1) * T // 2]
                                     .rearrange("o (j p) d -> p (o j) d", p=P)).then_inc(x1_in, 16)
                    rows = out.rearrange("b (c s) d -> b s c d", s=L)[bass.ds(b, 1)]
                    for j in range(JT):
                        sp.wait_ge(finished, b * JT + (j + 1))
                        for s2 in range(2):
                            sp.dma_start(rows[0, 2 * j + s2], last[s2 * C:(s2 + 1) * C, j, :]).then_inc(out_in, 16)
                sp.wait_ge(out_in, 16 * 2 * JT * B)

            @block.gpsimd
            def _(pool):
                g = nc.gpsimd

                def weigh(n, link):
                    for h in range(2):
                        g_w = gate_v[:, 2 * n:2 * n + 2, h, :].unsqueeze(3).to_broadcast([P, 2, E, DH])
                        link(g.tensor_tensor(mixed[:], xv_c[:, n % 2], g_w, ALU.mult))
                        to = v_next[:, 2 * n:2 * n + 2, h, :]
                        for e in range(1, E):
                            left = mixed[:, :, 0, :] if e == 1 else to
                            ins = g.tensor_tensor(to, left, mixed[:, :, e, :], ALU.add)
                            if h == 0 or e < E - 1:
                                link(ins)
                    ins.then_inc(v_mixed, 1)

                def mix(u, link):
                    for i in range(2):
                        j = 2 * u + i
                        link(g.tensor_tensor(mixed[:], o_rows[:, u % 2, i].unsqueeze(2).to_broadcast([P, 2, E, DH]),
                                             gate_o[:, j].unsqueeze(3).to_broadcast([P, 2, E, DH]), ALU.mult))
                        link(g.tensor_tensor(acc[:, j], acc[:, j], mixed[:, 0], ALU.add))
                        ins = g.tensor_tensor(acc[:, j], acc[:, j], mixed[:, 1], ALU.add)
                        if i == 0:
                            link(ins)
                    ins.then_inc(gated, 1)

                total = [0]

                def link0(ins):
                    total[0] += 1
                    ins.then_inc(pool_chain, 1)
                    pool.wait_ge(pool_chain, total[0])

                g.memset(mixed[:], 0.0).then_inc(gated, 2)
                pool.wait_ge(gated, 2)
                link0(g.tensor_copy(gate_v[:], gates[:, 0:JT, 0:2, :]))
                for n in range(UNITS):
                    pool.wait_ge(xv_in[n % 2], 16 * (n // 2 + 1))
                    weigh(n, link0)
                    pool.wait_ge(v_mixed, n + 1)
                before = total[0]

                LINKS = 2 + 9 * UNITS + 5 * UNITS
                with pool.Fori(0, B) as b:
                    with pool.Fori(0, PAIRS) as hp:
                        wait = counts(pool, b, hp)
                        following = (b * PAIRS + hp + 1) % (B * PAIRS)
                        seq, pair = pool.snap(following // PAIRS), pool.snap(following % PAIRS)
                        done = [0]

                        def link(ins):
                            done[0] += 1
                            ins.then_inc(pool_chain, 1)
                            wait(pool_chain, done[0], LINKS, 0, before)

                        link(g.tensor_copy(gate_o[:], gates[:, bass.ds(b * JT, JT),
                                                            bass.ds(hp * 2 + H, 2), :]))
                        link(g.tensor_copy(gate_v[:], gates[:, bass.ds(seq * JT, JT),
                                                            bass.ds(pair * 2, 2), :]))
                        wait(v_in, 16, 16)
                        for n in range(UNITS + 2):
                            if n < UNITS:
                                wait(xv_in[n % 2], 16 * (n // 2 + 1), 16 * UNITS // 2, 0, 16 * UNITS // 2)
                                weigh(n, link)
                                wait(v_mixed, n + 1, UNITS, 0, UNITS)
                            if n >= 2:
                                u = n - 2
                                if u == 0:
                                    pool.wait_ge(acc_zero, b + 1)
                                dve_copied(wait, ("o", u))
                                mix(u, link)
                                wait(gated, u + 1, UNITS, 0, 2)
                        assert done[0] == LINKS

            @block.vector
            def _(eng):
                v = nc.vector

                def low_parts(n, src):
                    c = n // 2
                    cs = slice(c * CH, (c + 1) * CH)
                    for h in range(2):
                        ps = slice(h * DH, (h + 1) * DH)
                        upper = q_s if n % 2 else k_hi
                        to = q_low[ps, c % 2, :] if n % 2 else k_lo[ps, h, cs]
                        ins = v.tensor_tensor(to, src[ps, :], upper[ps, h, cs].bitcast(F32), ALU.subtract)
                    ins.then_inc(dve_out, 1)

                for n in range(FIRST):
                    eng.wait_ge(act_out, n + 1)
                    if n % 2 and n >= 4:
                        eng.wait_ge(q_in[n // 2 - 2], 32)
                    low_parts(n, ring[n % 2])

                with eng.Fori(0, B) as b:
                    eng.wait_ge(used, b * (PAIRS * N_USE + JT) + FIRST)
                    v.memset(acc[:], 0.0).then_inc(acc_zero, 1)
                    with eng.Fori(0, PAIRS) as hp:
                        wait = counts(eng, b, hp)

                        def scores_out(r, c2):
                            wait(scored, 2 * r + c2 + 1, 2 * ROWS)
                            if c2 == 0 and r >= PBUF:
                                used_by(wait, ("t", r - PBUF, 3))
                            if c2 == 1:
                                wait(s_out, 2 * r + 1, 2 * ROWS)
                            v.tensor_scalar(probs[:, r % PBUF, c2 * T // 2:(c2 + 1) * T // 2], s_ps[c2][:],
                                            -SCALE, least[:, r, 0:1] if c2 else None, ALU.mult, ALU.min,
                                            accum_out=least[:, r, c2:c2 + 1]).then_inc(s_out, 1)

                        def rows_out(u):
                            wait(exp_out, 4 * u + 4, ROWS)
                            v.tensor_tensor(inv[:], sums[:, 4 * u:4 * u + 4, 0], sums[:, 4 * u:4 * u + 4, 1],
                                            ALU.add).then_inc(dve, 1)
                            wait(dve, 2 * u + 1, 2 * UNITS)
                            v.reciprocal(inv[:], inv[:]).then_inc(dve, 1)
                            wait(dve, 2 * u + 2, 2 * UNITS)
                            used_by(wait, ("o", u))
                            wait(gated, u - 1, UNITS, 0, 2)
                            v.tensor_tensor(o_rows[:, u % 2].rearrange("p i h d -> p (i h) d"),
                                            ring[USE["o", u] % 2][:, 0:2 * P].rearrange("p (n d) -> p n d", d=DH),
                                            inv[:].unsqueeze(2).to_broadcast([P, 4, DH]), ALU.mult
                                            ).then_inc(dve_out, 1)

                        for slot in range(SLOTS + 1):
                            r, t = slot, transposes_in(slot)
                            if r < ROWS:
                                scores_out(r, 0)
                            if t is not None:
                                used_by(wait, ("t", t, 1))
                                u = t // 4
                                if u >= 2:
                                    wait(av_done, u - 1, UNITS)
                                v.tensor_copy(probs_t[:, u % 2, 4:8, t % 2, (t // 2 % 2) * P:(t // 2 % 2 + 1) * P],
                                              ring[USE["t", t, 1] % 2][:].rearrange("p (j n) -> p j n", n=P)
                                              ).then_inc(dve_out, 1)
                            if r < ROWS:
                                scores_out(r, 1)
                            for n in projections_in(slot):
                                act_copied(wait, ("p", n))
                                if n % 2 and n >= 4:
                                    wait(q_in[n // 2 - 2], 32, 32, 0, 32)
                                low_parts(n, ring[USE["p", n] % 2])
                            if output_in(slot) is not None:
                                rows_out(output_in(slot))
                    eng.wait_ge(x1_in, b * 32 + 32)
                    for j in range(JT):
                        eng.wait_ge(projected, b * JT + (j + 1))
                        v.tensor_tensor(last[:, j, :], av[j % 2][:, 0:D], last[:, j, :], ALU.add
                                        ).then_inc(finished, 1)
                    eng.wait_ge(out_in, b * (32 * JT) + 32 * JT)

            @block.tensor
            def _(pe):
                mm = nc.tensor.matmul

                def project(n, bank, chunk_loads):
                    for k in range(DC):
                        ins = mm(bank[:], w_pair[:, k, n % 2, :], xc[:, n // 2 % 2, k, :], start=(k == 0),
                                 stop=(k == DC - 1))
                    ins.then_inc(used, 1)

                pe.wait_ge(w_in, 32)
                for n in range(FIRST):
                    pe.wait_ge(x_in[n // 2 % 2], 16 * (n // 4 + 1))
                    if n >= 2:
                        pe.wait_ge(dve_out, n - 1)
                    project(n, ring[n % 2], None)
                with pe.Fori(0, B) as b:
                    with pe.Fori(0, PAIRS) as hp:
                        wait = counts(pe, b, hp)

                        def bank_of(key):
                            n = USE[key]
                            if n >= 2:
                                copied(wait, NUMBER[n - 2])
                            elif n == 0:
                                wait(dve_out, 0, N_DVE, 0, FIRST)
                                wait(act_out, 0, N_ACT, JT, FIRST)
                            return ring[n % 2]

                        def scores(r, c2):
                            h, i = r % 2, r // 2
                            if r == 0:
                                pass
                            if r % 8 == 0 and c2 == 0:
                                wait(q_in[r // 8], 32, 32)
                            if r >= 1:
                                wait(s_out, 2 * (r - 1) + c2 + 1, 2 * ROWS)
                            for c in range(2 * c2, 2 * c2 + 2):
                                if r == 0:
                                    wait(k_in[c], 64, 64)
                                to = s_ps[c2][:, (c % 2) * CH:(c % 2 + 1) * CH]
                                q = q_s[:, h, i * P:(i + 1) * P]
                                mm(to, q, k_hi[:, h, c * CH:(c + 1) * CH], start=True, stop=False)
                                ins = mm(to, q, k_lo[:, h, c * CH:(c + 1) * CH], start=False, stop=True)
                            ins.then_inc(scored, 1)

                        def transposes(t, g):
                            to = bank_of(("t", t, g))
                            wait(exp_out, t + 1, ROWS)
                            for n in range(4):
                                ins = nc.tensor.transpose(to[:, n * P:(n + 1) * P],
                                                          probs[:, t % PBUF, (4 * g + n) * P:(4 * g + n + 1) * P],
                                                          ident[:])
                            ins.then_inc(used, 1)

                        def product(u, part, half):
                            if part == 0 and half == 0:
                                act_copied(wait, ("t", 4 * u + 3, 3))
                                dve_copied(wait, ("t", 4 * u + 3, 1))
                                if u == 0:
                                    wait(v_in, 16, 16)
                                if u >= 2:
                                    wait(av_out, u - 1, UNITS)
                            for j in range(part * AV_STEPS + half * 2, part * AV_STEPS + half * 2 + 2):
                                for h in range(2):
                                    ins = mm(av[u % 2][h * DH:(h + 1) * DH, 0:2 * P], v_sb[:, j, h, :],
                                             probs_t[:, u % 2, j, h, :], start=(j == 0), stop=(j == JT - 1))
                            if part == 3 and half == 1:
                                ins.then_inc(av_done, 1)

                        for slot in range(SLOTS + 1):
                            r, t = slot, transposes_in(slot)
                            u, part = product_in(slot)
                            if r < ROWS:
                                scores(r, 0)
                            if t is not None:
                                transposes(t, 0)
                            if u is not None:
                                product(u, part, 0)
                            if t is not None:
                                transposes(t, 1)
                            if r < ROWS:
                                scores(r, 1)
                            if t is not None:
                                transposes(t, 2)
                            if u is not None:
                                product(u, part, 1)
                            if t is not None:
                                transposes(t, 3)
                            for n in projections_in(slot):
                                bank = bank_of(("p", n))
                                if n == 0:
                                    wait(w_in, 32, 32, 0, 32)
                                if n % 2 == 0:
                                    wait(x_in[n // 2 % 2], 16 * (n // 4 + 1), 32, 0, 32)
                                project(n, bank, None)
                            if output_in(slot) is not None:
                                ou = output_in(slot)
                                bank = bank_of(("o", ou))
                                wait(av_out, ou + 1, UNITS)
                                for i in range(2):
                                    ins = nc.tensor.transpose(bank[:, i * P:(i + 1) * P],
                                                              o_t[:, ou % 2, i * P:(i + 1) * P], ident[:])
                                ins.then_inc(used, 1)
                    pe.wait_ge(wo_in, 32)
                    pe.wait_ge(gated, b * (PAIRS * UNITS) + (PAIRS * UNITS + 2))
                    pe.wait_ge(dve_out, b * (PAIRS * N_DVE) + (PAIRS * N_DVE + FIRST))
                    pe.wait_ge(av_out, b * (PAIRS * UNITS) + PAIRS * UNITS)
                    for j in range(JT + 1):
                        if j < JT:
                            if j >= 2:
                                pe.wait_ge(act_out, b * (PAIRS * N_ACT + JT) + (PAIRS * N_ACT + FIRST + j - 1))
                            a = acc[:, j].rearrange("p e d -> p (e d)")
                            for c in range(3):
                                w = P if c < 2 else DH
                                ins = nc.tensor.transpose(ring[j % 2][0:w, c * P:(c + 1) * P],
                                                          a[:, c * P:c * P + w], ident[:])
                            ins.then_inc(used, 1)
                        if j >= 1:
                            i = j - 1
                            pe.wait_ge(act_out, b * (PAIRS * N_ACT + JT) + (PAIRS * N_ACT + FIRST + i + 1))
                            if i >= 2:
                                pe.wait_ge(finished, b * JT + (i - 1))
                            for c in range(3):
                                w = P if c < 2 else DH
                                ins = mm(av[i % 2][:, 0:D], acc_t[0:w, i % 2, c, :], wo_sb[0:w, c, :],
                                         start=(c == 0), stop=(c == 2))
                            ins.then_inc(projected, 1)

            @block.scalar
            def _(act):
                a = nc.scalar.activation

                def upper_parts(n, src):
                    cs = slice(n // 2 * CH, (n // 2 + 1) * CH)
                    for h in range(2):
                        ps = slice(h * DH, (h + 1) * DH)
                        ins = a((q_s if n % 2 else k_hi)[ps, h, cs], src[ps, :], ACT.Copy)
                    ins.then_inc(act_out, 1)

                for n in range(FIRST):
                    act.wait_ge(used, n + 1)
                    upper_parts(n, ring[n % 2])
                with act.Fori(0, B) as b:
                    with act.Fori(0, PAIRS) as hp:
                        wait = counts(act, b, hp)

                        def exponentials(r, half):
                            if half == 0:
                                wait(s_out, 2 * r + 2, 2 * ROWS)
                            x = probs[:, r % PBUF, half * T // 2:(half + 1) * T // 2]
                            ins = a(x, x, ACT.Exp, bias=least[:, r, 1:2], scale=-1.0,
                                    accum_out=sums[:, r, half:half + 1])
                            if half:
                                ins.then_inc(exp_out, 1)

                        def transposed_out(t, g):
                            used_by(wait, ("t", t, g))
                            u = t // 4
                            if u >= 2:
                                wait(av_done, u - 1, UNITS)
                            a(probs_t[:, u % 2, 4 * g:4 * g + 4, t % 2, (t // 2 % 2) * P:(t // 2 % 2 + 1) * P],
                              ring[USE["t", t, g] % 2][:].rearrange("p (j n) -> p j n", n=P), ACT.Copy
                              ).then_inc(act_out, 1)

                        for slot in range(SLOTS + 1):
                            r, t = slot - 1, transposes_in(slot)
                            if 0 <= r < ROWS:
                                exponentials(r, 0)
                            if t is not None:
                                transposed_out(t, 0)
                            if 0 <= r < ROWS:
                                exponentials(r, 1)
                            if output_in(slot) is not None:
                                u = output_in(slot)
                                wait(av_done, u + 1, UNITS)
                                if u >= 2:
                                    used_by(wait, ("o", u - 2))
                                a(o_t[:, u % 2, :], av[u % 2][:, 0:2 * P], ACT.Copy).then_inc(av_out, 1)
                            if t is not None:
                                transposed_out(t, 2)
                                transposed_out(t, 3)
                            for n in projections_in(slot):
                                used_by(wait, ("p", n))
                                upper_parts(n, ring[USE["p", n] % 2])
                    for j in range(JT):
                        act.wait_ge(used, b * (PAIRS * N_USE + JT) + (PAIRS * N_USE + FIRST + j + 1))
                        if j >= 2:
                            act.wait_ge(projected, b * JT + (j - 1))
                        a(acc_t[:, j % 2, 0:2, :], ring[j % 2][:, 0:2 * P].rearrange("p (c n) -> p c n", c=2), ACT.Copy)
                        a(acc_t[0:DH, j % 2, 2, :], ring[j % 2][0:DH, 2 * P:3 * P], ACT.Copy).then_inc(act_out, 1)


_INS = ["x", "wi_t", "wh_t", "bi", "bh", "wq", "wk", "w_tok", "wo"]


def kernel(L0_attn_x, L0_attn_Wi, L0_attn_bi, L0_attn_Wh, L0_attn_bh, L0_ffn_Wq, L0_ffn_Wk, L0_ffn_Ws,
           L0_ffn_Wd, L0_ffn_Wv, L0_ffn_Wo):
    import numpy as np
    import concourse.bacc as bacc
    from concourse.bass_utils import run_bass_kernel_spmd

    arrays = {
        "x": L0_attn_x,
        "wi_t": np.transpose(L0_attn_Wi),
        "wh_t": np.transpose(L0_attn_Wh),
        "bi": np.transpose(np.reshape(L0_attn_bi, (DC, P))),
        "bh": np.transpose(np.reshape(L0_attn_bh, (DC, P))),
        "wq": L0_ffn_Wq,
        "wk": L0_ffn_Wk,
        "w_tok": np.concatenate([np.reshape(np.transpose(L0_ffn_Wv, (1, 0, 2)), (D, XV)), L0_ffn_Ws, L0_ffn_Wd],
                                axis=1),
        "wo": np.reshape(L0_ffn_Wo, (XV, D)),
    }
    arrays = {k: np.ascontiguousarray(v) for k, v in arrays.items()}
    nc = bacc.Bacc("TRN2", target_bir_lowering=False, num_devices=1, dynamic_dma_scratch_size=1024)
    args = [nc.dram_tensor(k, arrays[k].shape, mybir.dt.from_np(arrays[k].dtype), kind="ExternalInput").ap()
            for k in _INS]
    out = nc.dram_tensor("out", [B, T, D], F32, kind="ExternalOutput").ap()
    build(nc, *args, out)
    r = run_bass_kernel_spmd(nc, [arrays], core_ids=[0])
    return r.results[0]["out"]
```

```python
from contextlib import ExitStack

import concourse.bass as bass
from concourse import mybir

F32 = mybir.dt.float32
F32R = mybir.dt.float32r
I32 = mybir.dt.int32
ALU = mybir.AluOpType
ACT = mybir.ActivationFunctionType
AX = mybir.AxisListType

P = 128
B, T, D = 2, 2048, 256
DC = D // P
H, DH, E, SEL = 8, 64, 5, 2
EPS = 1e-5

C = P // B
L = T // C
WARM = 16
TOLERANCE = 2.0 ** -21

JT = T // P
XV = E * DH
GL = 2 * H * E
PAIRS = H // 2


def build(nc, x, wi_t, wh_t, bi, bh, wq, wk, w_tok, wo, out):
    dram = {
        name: nc.dram_tensor(name, shape, F32, kind="Internal").ap()
        for name, shape in (
            ("x1_dram", [B, T, D]),
            ("x2t_dram", [P, DC, B, T]),
            ("xv_dram", [B, JT, P, XV]),
        )
    }
    with ExitStack() as ctx:
        ident = ctx.enter_context(nc.sbuf_tensor("ident", [P, P], F32))
        gates = ctx.enter_context(nc.sbuf_tensor("gates", [P, B * JT, 2 * H, E], F32))
        prepare(nc, dram, x, wi_t, wh_t, bi, bh, w_tok, ident, gates)
        attend(nc, dram, wq, wk, wo, ident, gates, out)


def rsqrt(v, link, y, var, tmp, tmp_bits, var_bits, y_bits):
    link(v.tensor_scalar(tmp_bits, var_bits, 1, None, ALU.logical_shift_right))
    link(v.tensor_scalar(y_bits, tmp_bits, -1.0, float(0x5F3759DF), ALU.mult, ALU.add))
    for _ in range(3):
        link(v.tensor_tensor(tmp, y, y, ALU.mult))
        link(v.tensor_tensor(tmp, tmp, var, ALU.mult))
        link(v.tensor_scalar(tmp, tmp, -0.5, 1.5, ALU.mult, ALU.add))
        link(v.tensor_tensor(y, y, tmp, ALU.mult))


def prepare(nc, dram, x, wi_t, wh_t, bi, bh, w_tok, ident, gates):
    with ExitStack() as ctx:
        def sb(name, shape, dt=F32):
            return ctx.enter_context(nc.sbuf_tensor(name, shape, dt))

        def psum(name):
            return ctx.enter_context(nc.psum_tensor(name, [P, 512], F32))

        def sem(name):
            return ctx.enter_context(nc.semaphore(name))

        x_sb = sb("x_sb", [P, L, D])
        xn = sb("xn", [P, L, D])
        xn_t = sb("xn_t", [P, DC, L, P])
        x2_t = xn_t[:].rearrange("p k s n -> p k (s n)").rearrange("p k (b n) -> p k b n", b=B)
        h_t = sb("h_t", [P, DC, L + 1, P])
        wi_sb = sb("wi_sb", [P, DC, D])
        wh_sb = sb("wh_sb", [P, DC, D])
        w_tok_sb = sb("w_tok_sb", [P, DC, XV + GL])
        bias2 = sb("bias2", [P, 2, DC])
        bias = sb("bias", [P, DC])
        st = sb("st", [P, L, 6])
        sm = sb("sm", [P, 7, L])
        mean, rstd, var = sm[:, 0, :], sm[:, 1, :], sm[:, 2, :]
        diff = sb("diff", [P, DC, B, C - 1])
        worst = sb("worst", [P, 1])
        worst_all = sb("worst_all", [1, 1])
        flag = sb("flag", [1, 1], I32)
        tok_sb = sb("tok_sb", [P, 2, XV])
        logit = sb("logit", [P, B * JT, 2 * H, E])
        rank = sb("rank", [P, B * JT, 2 * H, E])
        above = sb("above", [P, B, L // 8 * 2 * H, E - 1])
        weight = sb("weight", [P, B * JT, H * E])
        z = [[psum(f"z{p}{m}") for m in range(DC)] for p in range(2)]
        tp = [psum(f"tp{p}") for p in range(2)]
        tk = [psum(f"tk{p}") for p in range(2)]

        x_in = [sem(f"x_in{g}") for g in range(4)]
        w_in, w_tok_in = sem("w_in"), sem("w_tok_in")
        ident_zero, ident_ok = sem("ident_zero"), sem("ident_ok")
        dve = sem("dve_chain")
        norm1, tp1, tp1_act, tp1_dve = sem("norm1"), sem("tp1"), sem("tp1_act"), sem("tp1_dve")
        bias_ok = sem("bias_ok")
        z_ready, h_ready = sem("z_ready"), sem("h_ready")
        started, mismatch, turned, flagged = sem("started"), sem("mismatch"), sem("turned"), sem("flagged")
        back, added, norm2_known, norm2 = sem("back"), sem("added"), sem("norm2_known"), sem("norm2")
        tp2, tp2_out = sem("tp2"), sem("tp2_out")
        tok, tok_out = sem("tok"), sem("tok_out")
        xv_stored, stored = [sem("xv_stored0"), sem("xv_stored1")], sem("stored")
        ranks_zero = sem("ranks_zero")

        x_rows = x.rearrange("b (c s) d -> (b c) s d", s=L)
        G = L // 4
        GROUPS = [2, 3, 0, 1]
        GJ = G // 2
        ROUTED = [(0, GJ), (GJ, 2 * GJ), (2 * GJ, 3 * GJ), (3 * GJ, JT - 1), (JT - 1, JT)]
        PARTS = [(0, G // 2), (G // 2, G), (G, 2 * G), (2 * G, 3 * G), (3 * G, L)]
        PAIR_ORDER = [j for g in GROUPS for j in range(g * G // 2, (g + 1) * G // 2)]
        count = [0]

        def logit_of(t):
            return logit[:, (t % B) * JT + t // B].rearrange("p g e -> p (g e)")

        def counted(ins):
            count[0] += 1
            ins.then_inc(dve, 1)

        def link(ins):
            counted(ins)
            nc.vector.wait_ge(dve, count[0])

        def statistics(lo, n):
            s = slice(lo, lo + n)
            v = nc.vector
            a, b2 = sm[:, 3, s], sm[:, 4, s]
            link(v.tensor_tensor(a, st[:, s, 1], st[:, s, 4], ALU.subtract))
            link(v.tensor_tensor(mean[:, s], st[:, s, 1], st[:, s, 4], ALU.add))
            link(v.tensor_tensor(b2, st[:, s, 2], st[:, s, 5], ALU.add))
            link(v.tensor_tensor(a, a, a, ALU.mult))
            link(v.tensor_scalar(mean[:, s], mean[:, s], 0.5, None, ALU.mult))
            link(v.tensor_scalar(b2, b2, 1.0 / D, EPS, ALU.mult, ALU.add))
            link(v.scalar_tensor_tensor(var[:, s], a, 0.25, b2, ALU.mult, ALU.add))
            rsqrt(v, link, rstd[:, s], var[:, s], a, a.bitcast(I32), var[:, s].bitcast(I32),
                  rstd[:, s].bitcast(I32))

        with nc.Block() as block:

            @block.sync
            def _(sp):
                for n, g in enumerate(GROUPS):
                    sp.dma_start(x_sb[:, g * G:(g + 1) * G, :], x_rows[:, g * G:(g + 1) * G, :]
                                 ).then_inc(x_in[n], 16)
                    if n == 0:
                        sp.dma_start(wi_sb[:], wi_t.rearrange("(k p) h -> p k h", p=P)).then_inc(w_in, 16)
                        sp.dma_start(wh_sb[:], wh_t.rearrange("(k p) h -> p k h", p=P)).then_inc(w_in, 16)
                        sp.dma_start(bias2[:, 0, :], bi).then_inc(w_in, 16)
                        sp.dma_start(bias2[:, 1, :], bh).then_inc(w_in, 16)
                sp.dma_start(w_tok_sb[:], w_tok.rearrange("(k p) n -> p k n", p=P)).then_inc(w_tok_in, 16)
                for g in range(4):
                    sp.wait_ge(added, (g + 1) * G)
                    for b in range(B):
                        sp.dma_start(dram["x1_dram"][b].rearrange("(s c) d -> c s d", c=C)[:, g * G:(g + 1) * G],
                                     x_sb[b * C:(b + 1) * C, g * G:(g + 1) * G, :]).then_inc(stored, 16)
                    for t in range(B * g * GJ, B * (g + 1) * GJ):
                        if t == B * (g + 1) * GJ - B:
                            sp.wait_ge(tp2_out, DC * (g + 1) * GJ)
                            for k in range(DC):
                                sp.dma_start(dram["x2t_dram"][:, k, :, g * GJ * P:(g + 1) * GJ * P],
                                             x2_t[:, k, :, g * GJ * P:(g + 1) * GJ * P]).then_inc(stored, 16)
                        sp.wait_ge(tok_out, 3 * t + 3)
                        sp.dma_start(dram["xv_dram"][t % B, t // B], tok_sb[:, t % 2, :]
                                     ).then_inc(xv_stored[t % 2], 16)
                sp.wait_ge(stored, 16 * 4 * (B + DC))
                for p in range(2):
                    sp.wait_ge(xv_stored[p], 16 * B * JT // 2)

            @block.gpsimd
            def _(pool):
                nc.gpsimd.memset(ident[:], 0.0).then_inc(ident_zero, 1)
                pool.wait_ge(ident_zero, 1)
                nc.gpsimd.affine_select(out=ident[:], in_=ident[:], compare_op=ALU.not_equal, fill=1.0,
                                        base=0, pattern=[[-1, P]], channel_multiplier=1).then_inc(ident_ok, 1)
                for e in range(E):
                    nc.gpsimd.memset(rank[:, :, :, e], float(e)).then_inc(ranks_zero, 1)
                for n, (lo, hi) in enumerate(PARTS):
                    pool.wait_ge(norm2_known, n + 1)
                    for s in range(lo, hi):
                        nc.gpsimd.tensor_scalar(xn[:, s, :], x_sb[:, s, :], mean[:, s:s + 1], rstd[:, s:s + 1],
                                                ALU.subtract, ALU.mult).then_inc(norm2, 1)

            @block.vector
            def _(dve_eng):
                v = nc.vector
                link(v.memset(h_t[:, :, 0, :], 0.0))

                for n, g in enumerate(GROUPS):
                    dve_eng.wait_ge(x_in[n], 16)
                    for s in range(g * G, (g + 1) * G):
                        counted(v.bn_stats(st[:, s, :], x_sb[:, s, :]))
                    dve_eng.wait_ge(dve, count[0])
                    statistics(g * G, G)
                    for s in range(g * G, (g + 1) * G):
                        v.tensor_scalar(xn[:, s, :], x_sb[:, s, :], mean[:, s:s + 1], rstd[:, s:s + 1],
                                        ALU.subtract, ALU.mult).then_inc(norm1, 1)
                    if n == 0:
                        dve_eng.wait_ge(w_in, 64)
                        v.tensor_tensor(bias[:], bias2[:, 0, :], bias2[:, 1, :], ALU.add).then_inc(bias_ok, 1)
                for n in range(2 * GJ + 1, 4 * GJ, 2):
                    dve_eng.wait_ge(tp1, n + 1)
                    v.tensor_copy(xn_t[:, :, 2 * PAIR_ORDER[n]:2 * PAIR_ORDER[n] + 2, :],
                                  tp[n % 2][:].rearrange("p (k s n) -> p k s n", k=DC, s=2)
                                  ).then_inc(tp1_dve, 1)

                def start_states(steps):
                    dve_eng.wait_ge(h_ready, 2 * steps)
                    for k in range(DC):
                        last = v.tensor_copy(
                            h_t[:, k, 0, :].rearrange("p (b c) -> p b c", b=B)[:, :, 1:C],
                            h_t[:, k, L, :].rearrange("p (b c) -> p b c", b=B)[:, :, 0:C - 1])
                        last.then_inc(started, 1)

                start_states(WARM)
                dve_eng.wait_ge(h_ready, 2 * (WARM + L))
                for k in range(DC):
                    link(v.tensor_tensor(diff[:, k],
                                         h_t[:, k, L, :].rearrange("p (b c) -> p b c", b=B)[:, :, 0:C - 1],
                                         h_t[:, k, 0, :].rearrange("p (b c) -> p b c", b=B)[:, :, 1:C],
                                         ALU.subtract))
                v.tensor_reduce(worst[:], diff[:].rearrange("p k b c -> p (k b c)"), AX.X, ALU.max,
                                apply_absolute_value=True).then_inc(mismatch, 1)
                dve_eng.wait_ge(turned, 1)
                link(v.tensor_reduce(worst_all[:], tk[0][0:1, 0:P], AX.X, ALU.max))
                v.tensor_scalar(flag[:], worst_all[:], TOLERANCE, None, ALU.is_gt).then_inc(flagged, 1)
                dve_eng.wait_ge(flagged, 1)
                again = v.value_load(flag[0:1, 0:1], min_val=0, max_val=1)
                with dve_eng.If(again == 1):
                    with dve_eng.Fori(0, C - 1) as r:
                        start_states(r * L + (WARM + L))
                    dve_eng.wait_ge(h_ready, 2 * (WARM + C * L))

                def route(part):
                    lo, hi = part
                    dve_eng.wait_ge(tok_out, 3 * B * hi)
                    lg, rk = [x[:].rearrange("p (b j) g e -> p b (j g) e", b=B)[:, :, lo * 2 * H:hi * 2 * H]
                              for x in (logit, rank)]
                    for d in range(1, E):
                        gt = above[:, :, 0:(hi - lo) * 2 * H, 0:E - d]
                        link(v.tensor_tensor(gt, lg[:, :, :, d:E], lg[:, :, :, 0:E - d], ALU.is_gt))
                        link(v.tensor_tensor(rk[:, :, :, 0:E - d], rk[:, :, :, 0:E - d], gt, ALU.add))
                        link(v.tensor_tensor(rk[:, :, :, d:E], rk[:, :, :, d:E], gt, ALU.subtract))
                    rows, to = [x[:].rearrange("p (b j) g e -> p b j (g e)", b=B)[:, :, lo:hi]
                                for x in (rank, gates)]
                    link(v.tensor_scalar(to, rows, SEL - 0.5, None, ALU.is_lt))
                    w = weight[:].rearrange("p (b j) n -> p b j n", b=B)[:, :, lo:hi]
                    link(v.tensor_scalar(w, w, 1.0, None, ALU.add))
                    link(v.reciprocal(w, w))
                    link(v.tensor_tensor(to[:, :, :, 0:H * E], to[:, :, :, 0:H * E], w, ALU.mult))

                dve_eng.wait_ge(ranks_zero, E)
                for n, (lo, hi) in enumerate(PARTS):
                    if n == len(PARTS) - 1:
                        route(ROUTED[0])
                    for s in range(lo, hi):
                        dve_eng.wait_ge(back, s + 1)
                        v.tensor_tensor(x_sb[:, s, :], tp[s % 2][:, 0:D], x_sb[:, s, :], ALU.add
                                        ).then_inc(added, 1)
                        if s > lo:
                            dve_eng.wait_ge(added, s)
                            counted(v.bn_stats(st[:, s - 1, :], x_sb[:, s - 1, :]))
                    dve_eng.wait_ge(added, hi)
                    link(v.bn_stats(st[:, hi - 1, :], x_sb[:, hi - 1, :]))
                    statistics(lo, hi - lo)
                    dve_eng.sem_inc(norm2_known, 1)
                for part in ROUTED[1:]:
                    route(part)

            @block.tensor
            def _(pe):
                def transpose_pair(n, j, normed, done):
                    for s2 in range(2):
                        for k in range(DC):
                            last = nc.tensor.transpose(
                                normed[n % 2][:, (2 * k + s2) * P:(2 * k + s2 + 1) * P],
                                xn[:, 2 * j + s2, k * P:(k + 1) * P], ident[:])
                    last.then_inc(done, 1)

                def transposes1(lo, hi):
                    for n in range(lo, hi):
                        pe.wait_ge(norm1, 2 * n + 2)
                        if n >= 2 and n - 2 < 2 * GJ:
                            pe.wait_ge(tp1_act, n - 1)
                        elif n >= 2 and n % 2 == 0:
                            pe.wait_ge(tp1_act, 2 * GJ + (n - 2 * GJ) // 2)
                        elif n >= 2:
                            pe.wait_ge(tp1_dve, (n - 2 * GJ) // 2)
                        transpose_pair(n, PAIR_ORDER[n], tp, tp1)

                def x_part(q, s, alone=False):
                    for m in range(DC):
                        for k in range(DC):
                            last = nc.tensor.matmul(z[q % 2][m][:, 0:P], wi_sb[:, k, m * P:(m + 1) * P],
                                                    xn_t[:, k, s, :], start=(k == 0),
                                                    stop=alone and k == DC - 1)
                        if alone:
                            last.then_inc(z_ready, 1)

                def h_part(parity, steps, slot):
                    for k in range(DC):
                        pe.wait_ge(h_ready, steps * 2 - 1 + k)
                        for m in range(DC):
                            last = nc.tensor.matmul(z[parity][m][:, 0:P], wh_sb[:, k, m * P:(m + 1) * P],
                                                    h_t[:, k, slot, :], start=False, stop=(k == DC - 1))
                            if k == DC - 1:
                                last.then_inc(z_ready, 1)

                def sweep(steps):
                    with pe.Fori(0, L // 2 - 1) as i:
                        h_part(0, i * 2 + steps, i * 2)
                        x_part(1, i * 2 + 1)
                        h_part(1, i * 2 + (steps + 1), i * 2 + 1)
                        x_part(0, i * 2 + 2)
                    h_part(0, steps + (L - 2), L - 2)
                    x_part(1, L - 1)
                    h_part(1, steps + (L - 1), L - 1)

                pe.wait_ge(ident_ok, 1)
                transposes1(0, GJ)
                pe.wait_ge(w_in, 64)
                pe.wait_ge(tp1_act, GJ)
                x_part(0, L - WARM, alone=True)
                x_part(1, L - WARM + 1)
                for lo, hi in ((0, GJ - 1), (GJ - 1, WARM // 2 - 1)):
                    if lo:
                        transposes1(GJ, 2 * GJ)
                        pe.wait_ge(tp1_act, 2 * GJ)
                    with pe.Fori(lo, hi) as i:
                        h_part(1, i * 2 + 1, i * 2 + (L - WARM + 1))
                        x_part(0, i * 2 + (L - WARM + 2))
                        h_part(0, i * 2 + 2, i * 2 + (L - WARM + 2))
                        x_part(1, i * 2 + (L - WARM + 3))
                h_part(1, WARM - 1, L - 1)
                transposes1(2 * GJ, 4 * GJ)
                pe.wait_ge(tp1_act, 3 * GJ)
                pe.wait_ge(tp1_dve, GJ)
                x_part(0, 0)
                pe.wait_ge(started, DC)
                sweep(WARM)
                pe.wait_ge(mismatch, 1)
                nc.tensor.transpose(tk[0][0:1, 0:P], worst[:], ident[:]).then_inc(turned, 1)
                pe.wait_ge(flagged, 1)
                again = nc.tensor.value_load(flag[0:1, 0:1], min_val=0, max_val=1)
                with pe.If(again == 1):
                    with pe.Fori(0, C - 1) as r:
                        x_part(0, 0)
                        pe.wait_ge(started, r * DC + 2 * DC)
                        for s in range(L):
                            h_part(s % 2, r * L + (WARM + L + s), s)
                            if s < L - 1:
                                x_part((s + 1) % 2, s + 1)
                    pe.wait_ge(h_ready, 2 * (WARM + C * L))
                pe.wait_ge(w_tok_in, 16)

                def back_to_rows(s):
                    if s >= 2:
                        pe.wait_ge(added, s - 1)
                    for k in range(DC):
                        last = nc.tensor.transpose(tp[s % 2][:, k * P:(k + 1) * P], h_t[:, k, s + 1, :],
                                                   ident[:])
                    last.then_inc(back, 1)

                def token_products(j):
                    pe.wait_ge(tp2_out, 2 * (j + 1))
                    for b in range(B):
                        t = 2 * j + b
                        if t >= 4:
                            pe.wait_ge(tok_out, 3 * (t - 3))
                        for k in range(DC):
                            last = nc.tensor.matmul(z[j % 2][b][:, 0:XV + GL], x2_t[:, k, b, j * P:(j + 1) * P],
                                                    w_tok_sb[:, k, :], start=(k == 0), stop=(k == DC - 1))
                        last.then_inc(tok, 1)

                pe.wait_ge(h_ready, 2 * (WARM + L))
                for n in range(len(PARTS) + 1):
                    if n < len(PARTS):
                        for s in range(*PARTS[n]):
                            back_to_rows(s)
                    if n > 0:
                        for j in range(PARTS[n - 1][0] // 2, PARTS[n - 1][1] // 2):
                            pe.wait_ge(norm2, 2 * j + 2)
                            if j >= 2:
                                pe.wait_ge(tp2_out, 2 * (j - 1))
                            transpose_pair(j, j, tk, tp2)
                            if j >= 1:
                                token_products(j - 1)
                token_products(JT - 1)

            @block.scalar
            def _(act):
                def transposed1(n):
                    act.wait_ge(tp1, n + 1)
                    nc.scalar.activation(xn_t[:, :, 2 * PAIR_ORDER[n]:2 * PAIR_ORDER[n] + 2, :],
                                         tp[n % 2][:].rearrange("p (k s n) -> p k s n", k=DC, s=2),
                                         ACT.Copy).then_inc(tp1_act, 1)

                for n in range(GJ):
                    transposed1(n)
                act.wait_ge(bias_ok, 1)

                def step(parity, steps, slot):
                    for m in range(DC):
                        act.wait_ge(z_ready, steps * 2 + m + 1)
                        nc.scalar.activation(h_t[:, m, slot, :], z[parity][m][:, 0:P], ACT.Tanh,
                                             bias=bias[:, m:m + 1]).then_inc(h_ready, 1)

                with act.Fori(0, GJ - 1) as i:
                    step(0, i * 2, i * 2 + (L - WARM + 1))
                    step(1, i * 2 + 1, i * 2 + (L - WARM + 2))
                step(0, G - 2, L - WARM + G - 1)
                for n in range(GJ, 2 * GJ):
                    transposed1(n)
                step(1, G - 1, L - WARM + G)
                with act.Fori(GJ, WARM // 2) as i:
                    step(0, i * 2, i * 2 + (L - WARM + 1))
                    step(1, i * 2 + 1, i * 2 + (L - WARM + 2))
                for n in range(2 * GJ, 4 * GJ, 2):
                    transposed1(n)
                with act.Fori(0, L // 2) as i:
                    step(0, i * 2 + WARM, i * 2 + 1)
                    step(1, i * 2 + (WARM + 1), i * 2 + 2)
                act.wait_ge(flagged, 1)
                again = nc.scalar.value_load(flag[0:1, 0:1], min_val=0, max_val=1)
                with act.If(again == 1):
                    with act.Fori(0, C - 1) as r:
                        for s in range(L):
                            step(s % 2, r * L + (WARM + L + s), s + 1)
                for j in range(JT + 1):
                    if j < JT:
                        act.wait_ge(tp2, j + 1)
                        for k in range(DC):
                            nc.scalar.activation(
                                x2_t[:, k, :, j * P:(j + 1) * P].rearrange("p b (s c) -> p b s c", s=2),
                                tk[j % 2][:, 2 * k * P:2 * (k + 1) * P].rearrange("p (s b c) -> p b s c", s=2, b=B),
                                ACT.Copy).then_inc(tp2_out, 1)
                    for b in range(B if j else 0):
                        t = 2 * (j - 1) + b
                        products = z[(j - 1) % 2][b]
                        act.wait_ge(tok, t + 1)
                        nc.scalar.activation(weight[:, b * JT + j - 1, :], products[:, XV:XV + H * E], ACT.Exp,
                                             scale=-1.0).then_inc(tok_out, 1)
                        nc.scalar.activation(logit_of(t), products[:, XV:XV + GL], ACT.Copy).then_inc(tok_out, 1)
                        if t >= 2:
                            act.wait_ge(xv_stored[t % 2], 16 * (t // 2))
                        nc.scalar.activation(tok_sb[:, t % 2, :], products[:, 0:XV], ACT.Copy
                                             ).then_inc(tok_out, 1)


SCALE = DH ** -0.5
CH = 512
NCH = T // CH
ROWS = 2 * JT
UNITS = JT // 2
PBUF = 3
LAG_T = 2
LAG_AV = 6
AV_STEPS = JT // 4

HEAD = LAG_AV
FIRST_SLOTS = range(0, HEAD)
OWN_SLOTS = range(HEAD, ROWS)
NEXT_SLOTS = range(ROWS, ROWS + HEAD)

DVE_UNITS = 3

QUERY_SLOT = {9: 0, 17: 1, 25: 2}

TURN_UNIT = UNITS - 2
TURN = [("k", 0), ("e", 0), ("k", 1), ("e", 1), ("k", 2), ("k", 3),
        ("t", ROWS - 2, 0), ("av", 2, 0), ("t", ROWS - 2, 1), ("t", ROWS - 2, 2), ("av", 2, 1), ("t", ROWS - 2, 3),
        ("t", ROWS - 1, 0), ("av", 3, 0), ("t", ROWS - 1, 1), ("t", ROWS - 1, 2), ("av", 3, 1), ("t", ROWS - 1, 3),
        ("q", 3)]
LAST_TURN = [op for op in TURN if op[0] not in ("k", "q")]
NO_QUERIES = [("q", 3)]
NO_ROWS = [[("t", ROWS + n, g) for n in rows for g in range(4)] for rows in ((0, 1, 2), (3,))]
AHEAD_OF_ALL = [*(("k", n) for n in range(NCH)), *(("q", n) for n in range(NCH))]


def transposes_in(slot):
    return None if slot < LAG_T or slot in (ROWS, ROWS + 1) else slot - LAG_T


def product_in(slot):
    if slot < HEAD or slot >= ROWS + 4:
        return None, None
    return (UNITS - 1, slot - ROWS) if slot >= ROWS else ((slot - HEAD) // 4, (slot - HEAD) % 4)


def output_in(slot):
    n = slot - LAG_AV - 4
    if slot == ROWS:
        return UNITS - 2
    if slot == ROWS + 4:
        return UNITS - 1
    return n // 4 if 0 <= n and slot < ROWS and n % 4 == 0 else None


def copier(t, g):
    two = t in (ROWS - 2, ROWS - 1) or product_in(t + LAG_T)[0] is None
    return "dve" if g == 1 or (g == 3 and two) else "act"


def buffer_of(r):
    return r % ROWS % PBUF


def former_row(r):
    return max(q for q in range(r) if buffer_of(q) == buffer_of(r))


class Ring:

    def __init__(self, slots, turn, before=None):
        self.use, self.act, self.dve = {}, {}, {}
        self.before = before.totals() if before else (0, 0, 0)
        for slot in slots:
            if slot in (0, ROWS):
                for op in turn:
                    if op[0] == "t":
                        self.add(op, copier(*op[1:]) == "act", copier(*op[1:]) == "dve")
                    elif op[0] == "q":
                        self.add(op, True, True)
            if transposes_in(slot) is not None:
                for g in range(4):
                    who = copier(transposes_in(slot), g)
                    self.add(("t", transposes_in(slot), g), who == "act", who == "dve")
            if slot in QUERY_SLOT:
                self.add(("q", QUERY_SLOT[slot]), True, True)
            if output_in(slot) is not None:
                self.add(("o", output_in(slot)), False, True)
        self.key = {n: key for key, n in self.use.items()}

    def add(self, key, act, dve):
        self.use[key] = len(self.use)
        if act:
            self.act[key] = len(self.act)
        if dve:
            self.dve[key] = len(self.dve)

    def totals(self):
        return len(self.use), len(self.act), len(self.dve)


def attend(nc, dram, wq, wk, wo, ident, gates, out):
    AHEAD = Ring(FIRST_SLOTS, AHEAD_OF_ALL)
    BODY = Ring([*OWN_SLOTS, *NEXT_SLOTS], TURN, before=AHEAD)
    A_USE, A_ACT, A_DVE = AHEAD.totals()
    N_USE, N_ACT, N_DVE = BODY.totals()
    assert A_USE % 2 == 0 and N_USE % 2 == 0
    with ExitStack() as ctx:
        def sb(name, shape, dt=F32):
            return ctx.enter_context(nc.sbuf_tensor(name, shape, dt))

        def psum(name, n):
            return ctx.enter_context(nc.psum_tensor(name, [P, n], F32))

        def sem(name):
            return ctx.enter_context(nc.semaphore(name))

        xc = sb("xc", [P, NCH, DC, CH])
        w_pair = sb("w_pair", [P, DC, 2, P])
        q_s = sb("q_s", [P, 2, T], F32R)
        k_s = sb("k_s", [P, 2, 2, T], F32R)
        q_low = sb("q_low", [P, 2, CH], F32R)
        probs = sb("probs", [P, PBUF, T])
        probs_t = sb("probs_t", [P, 2, JT, 2, 2 * P])
        least = sb("least", [P, ROWS, 2])
        sums = sb("sums", [P, ROWS, 2])
        inv = sb("inv", [P, 4])
        v_sb = sb("v_sb", [P, JT, 2, DH])
        v_next = sb("v_next", [P, JT, 2, DH])
        xv_c = sb("xv_c", [P, 2, 2, E, DH])
        gate_v = sb("gate_v", [P, JT, 2, E])
        gate_o = sb("gate_o", [P, JT, 2, E])
        mixed = sb("mixed", [P, 2, E, DH])
        o_t = sb("o_t", [P, 2, 2 * P])
        o_rows = sb("o_rows", [P, 2, 2, 2, DH])
        acc = sb("acc", [P, JT, E, DH])
        wo_sb = sb("wo_sb", [P, 3, D])
        s_ps = [psum(f"s_ps{c}", 2 * CH) for c in range(2)]
        ring = [psum(f"ring{p}", CH) for p in range(2)]
        av = [psum(f"av{p}", CH) for p in range(2)]
        acc_t = q_low[:].bitcast(F32).rearrange("p a n -> p (a n)")[:, 0:2 * 3 * P].rearrange(
            "p (a c n) -> p a c n", a=2, c=3)
        last = xc[:].rearrange("p c k n -> p (c k n)").rearrange("p (j d) -> p j d", d=D)

        x_in, w_in, wo_in = [sem(f"x_in_{c}") for c in range(NCH)], sem("w_pair_in"), sem("wo_in")
        used, act_out, dve_out = sem("used"), sem("act_out"), sem("dve_out")
        keys, keys_upper, keys_lower = sem("keys"), sem("keys_upper"), sem("keys_lower")
        k_in, q_in = [sem(f"k_in{c}") for c in range(NCH // 2)], [sem(f"q_in{c}") for c in range(NCH)]
        scored, s_out, exp_out = sem("scored"), sem("s_out"), sem("exp_out")
        av_done, av_out = sem("av_done"), sem("av_out")
        xv_in, v_mixed, v_in = [sem("xv_in0"), sem("xv_in1")], sem("v_mixed"), sem("v_in")
        dve, dve_first, pool_chain = sem("dve_chain2"), sem("dve_chain_first"), sem("pool_chain")
        gated, acc_zero = sem("gated"), sem("acc_zero")
        xv_first, first_gates = [sem(f"xv_first{n}") for n in range(UNITS)], sem("first_gates")
        first_mixed, first_mixed_dve = sem("first_mixed"), sem("first_mixed_dve")

        def experts_first(n):
            flat = probs[:].rearrange("p a n -> p (a n)")
            return flat[:, 2 * n * XV:2 * (n + 1) * XV].rearrange("p (j e k) -> p j e k", j=2, e=E)
        x1_in, projected, finished, out_in = sem("x1_in"), sem("projected"), sem("finished"), sem("out_in")

        def weigh(e, n, link, experts, to, scratch):
            for h in range(2):
                g_w = gate_v[:, 2 * n:2 * n + 2, h, :].unsqueeze(3).to_broadcast([P, 2, E, DH])
                link(e.tensor_tensor(scratch, experts, g_w, ALU.mult))
                out_h = to[:, 2 * n:2 * n + 2, h, :]
                for k in range(1, E):
                    left = scratch[:, :, 0, :] if k == 1 else out_h
                    ins = e.tensor_tensor(out_h, left, scratch[:, :, k, :], ALU.add)
                    if h == 0 or k < E - 1:
                        link(ins)
            return ins

        def keys_bank(n):
            return s_ps[n // 2][:, (n % 2) * CH:(n % 2 + 1) * CH]

        class Counts:

            def __init__(self, eng, ring_no, b=None, hp=None):
                self.eng, self.ring, self.b = eng, ring_no, b
                self.p = None if b is None else b * PAIRS + hp

            def wait(self, semaphore, n, per_pair, per_seq=0, before=0):
                v = n + before
                if self.p is not None:
                    v = self.p * per_pair + v
                    if per_seq:
                        v = v + self.b * per_seq
                self.eng.wait_ge(semaphore, v)

            def of_turn(self, semaphore, n, each):
                self.wait(semaphore, n, each, 0, 0 if self.p is None else each)

            def goes_on(self):
                return self.p < B * PAIRS - 1

            def ends(self):
                return self.p == B * PAIRS - 1

            def passed(self, semaphore, numbers, keys):
                n = len([k for k in keys if k in numbers])
                if n:
                    self.eng.drain().then_inc(semaphore, n)

            def used(self, key):
                self.wait(used, self.ring.use[key] + 1, N_USE, JT, self.ring.before[0])

            def act_copied(self, key):
                self.wait(act_out, self.ring.act[key] + 1, N_ACT, JT, self.ring.before[1])

            def dve_copied(self, key):
                self.wait(dve_out, self.ring.dve[key] + 1, N_DVE, 0, self.ring.before[2])

            def copied(self, key):
                if key in self.ring.dve:
                    self.dve_copied(key)
                else:
                    self.act_copied(key)

            def row_copied(self, t):
                self.act_copied(("t", t, 2 if copier(t, 3) == "dve" else 3))
                self.dve_copied(("t", t, 3 if copier(t, 3) == "dve" else 1))

        with nc.Block() as block:

            @block.sync
            def _(sp):
                def load_weights(head_pair):
                    for n, w in enumerate((wk, wq)):
                        sp.dma_start(w_pair[:, :, n, :],
                                     w.rearrange("(k p) n -> p k n", p=P)[:, :, bass.ds(head_pair * P, P)]
                                     ).then_inc(w_in, 16)

                def load_chunk(seq, c):
                    sp.dma_start(xc[:, c], dram["x2t_dram"][:, :, bass.ds(seq, 1), c * CH:(c + 1) * CH]
                                 .rearrange("p k o n -> p k (o n)")).then_inc(x_in[c], 16)

                def load_values(seq, n):
                    sp.dma_start(xv_c[:, n % 2],
                                 dram["xv_dram"][bass.ds(seq, 1), 2 * n:2 * n + 2]
                                 .rearrange("o j p (e k) -> p (o j) e k", e=E)).then_inc(xv_in[n % 2], 16)

                top, bottom = slice(0, DH), slice(DH, P)
                OTHER_HALVES = ((0, bottom, top), (1, top, bottom))

                def lower_queries(c, n):
                    c.dve_copied(("q", n))
                    cs = slice(n * CH, (n + 1) * CH)
                    for h, to, of in OTHER_HALVES:
                        sp.dma_start(q_s[to, h, cs].bitcast(F32), q_low[of, n % 2, :].bitcast(F32)
                                     ).then_inc(q_in[n], 16)

                def twice_keys(c, n):
                    c.of_turn(keys_lower, 2 * n + 2, NCH)
                    cs = slice(2 * n * CH, 2 * (n + 1) * CH)
                    for h, to, of in OTHER_HALVES:
                        sp.dma_start(k_s[to, :, h, cs].bitcast(F32), k_s[of, :, h, cs].bitcast(F32)
                                     ).then_inc(k_in[n], 16)

                load_weights(0)
                load_chunk(0, 0)
                for i, n in enumerate((0, DVE_UNITS, *range(1, DVE_UNITS), *range(DVE_UNITS + 1, UNITS))):
                    if i in (1, 2):
                        load_chunk(0, i)
                    sp.dma_start(experts_first(n), dram["xv_dram"][0, 2 * n:2 * n + 2]
                                 .rearrange("j p (e k) -> p j e k", e=E)).then_inc(xv_first[n], 16)
                load_chunk(0, NCH - 1)
                sp.dma_start(wo_sb[:, 0:2, :], wo[0:2 * P].rearrange("(c p) d -> p c d", p=P)).then_inc(wo_in, 16)
                sp.dma_start(wo_sb[0:DH, 2, :], wo[2 * P:XV]).then_inc(wo_in, 16)
                c = Counts(sp, AHEAD)
                for n in range(NCH // 2):
                    twice_keys(c, n)
                for n in range(NCH):
                    lower_queries(c, n)

                with sp.Fori(0, B) as b:
                    with sp.Fori(0, PAIRS) as hp:
                        c = Counts(sp, BODY, b, hp)
                        following = (b * PAIRS + hp + 1) % (B * PAIRS)
                        seq, pair = sp.snap(following // PAIRS), sp.snap(following % PAIRS)
                        for n in range(UNITS):
                            if n >= 2:
                                c.wait(v_mixed, n - 1, UNITS)
                            load_values(seq, n)
                            if n == 1:
                                load_weights(pair)
                                sp.wait_ge(out_in, b * (32 * JT) + 16)
                                for chunk in range(NCH):
                                    load_chunk(seq, chunk)
                            if n in (4, 6, 7):
                                lower_queries(c, {4: 0, 6: 1, 7: 2}[n])
                        with sp.If(c.goes_on()):
                            for n in range(NCH // 2):
                                twice_keys(c, n)
                            lower_queries(c, NCH - 1)
                        c.wait(v_mixed, UNITS, UNITS)
                        c.wait(av_done, UNITS, UNITS)
                        sp.dma_start(v_sb[:], v_next[:]).then_inc(v_in, 16)
                    for n in range(2):
                        sp.dma_start(last[:, 8 * n:8 * n + 8, :],
                                     dram["x1_dram"][bass.ds(b, 1), n * T // 2:(n + 1) * T // 2]
                                     .rearrange("o (j p) d -> p (o j) d", p=P)).then_inc(x1_in, 16)
                    rows = out.rearrange("b (c s) d -> b s c d", s=L)[bass.ds(b, 1)]
                    for j in range(JT):
                        sp.wait_ge(finished, b * JT + (j + 1))
                        for s2 in range(2):
                            sp.dma_start(rows[0, 2 * j + s2], last[s2 * C:(s2 + 1) * C, j, :]).then_inc(out_in, 16)
                sp.wait_ge(out_in, 16 + 32 * JT * B)

            @block.gpsimd
            def _(pool):
                g = nc.gpsimd

                def mix(u, link):
                    for i in range(2):
                        j = 2 * u + i
                        link(g.tensor_tensor(mixed[:], o_rows[:, u % 2, i].unsqueeze(2).to_broadcast([P, 2, E, DH]),
                                             gate_o[:, j].unsqueeze(3).to_broadcast([P, 2, E, DH]), ALU.mult))
                        link(g.tensor_tensor(acc[:, j], acc[:, j], mixed[:, 0], ALU.add))
                        ins = g.tensor_tensor(acc[:, j], acc[:, j], mixed[:, 1], ALU.add)
                        if i == 0:
                            link(ins)
                    ins.then_inc(gated, 1)

                total = [0]

                def link0(ins):
                    total[0] += 1
                    ins.then_inc(pool_chain, 1)
                    pool.wait_ge(pool_chain, total[0])

                g.memset(mixed[:, 0], 0.0).then_inc(gated, 2)
                g.memset(mixed[:, 1], 0.0).then_inc(out_in, 16)
                pool.wait_ge(gated, 2)
                pool.wait_ge(out_in, 16)
                g.tensor_copy(gate_v[:], gates[:, 0:JT, 0:2, :]).then_inc(first_gates, 1)
                pool.wait_ge(first_gates, 1)
                for i, n in enumerate(range(DVE_UNITS, UNITS)):
                    pool.wait_ge(xv_first[n], 16)
                    weigh(g, n, link0, experts_first(n), v_sb, mixed[:]).then_inc(first_mixed, 1)
                    pool.wait_ge(first_mixed, i + 1)
                pool.sem_inc(v_in, 8)
                pool.wait_ge(first_mixed_dve, DVE_UNITS)
                before = total[0]

                LINKS = 2 + 9 * UNITS + 5 * UNITS
                with pool.Fori(0, B) as b:
                    with pool.Fori(0, PAIRS) as hp:
                        c = Counts(pool, BODY, b, hp)
                        following = (b * PAIRS + hp + 1) % (B * PAIRS)
                        seq, pair = pool.snap(following // PAIRS), pool.snap(following % PAIRS)
                        done = [0]

                        def link(ins):
                            done[0] += 1
                            ins.then_inc(pool_chain, 1)
                            c.wait(pool_chain, done[0], LINKS, 0, before)

                        link(g.tensor_copy(gate_o[:], gates[:, bass.ds(b * JT, JT),
                                                            bass.ds(hp * 2 + H, 2), :]))
                        link(g.tensor_copy(gate_v[:], gates[:, bass.ds(seq * JT, JT),
                                                            bass.ds(pair * 2, 2), :]))
                        c.wait(v_in, 16, 16)
                        for n in range(UNITS + 2):
                            if n < UNITS:
                                c.wait(xv_in[n % 2], 16 * (n // 2 + 1), 16 * UNITS // 2)
                                weigh(g, n, link, xv_c[:, n % 2], v_next, mixed[:]).then_inc(v_mixed, 1)
                                c.wait(v_mixed, n + 1, UNITS)
                            if n >= 2:
                                u = n - 2
                                if u == 0:
                                    pool.wait_ge(acc_zero, b + 1)
                                c.dve_copied(("o", u))
                                mix(u, link)
                                c.wait(gated, u + 1, UNITS, 0, 2)
                        assert done[0] == LINKS

            @block.vector
            def _(eng):
                v = nc.vector

                def lower_keys(c, n):
                    c.of_turn(keys_upper, n + 1, NCH)
                    cs = slice(n * CH, (n + 1) * CH)
                    for h in range(2):
                        ps = slice(h * DH, (h + 1) * DH)
                        ins = v.tensor_tensor(k_s[ps, 1, h, cs], keys_bank(n)[ps, :], k_s[ps, 0, h, cs].bitcast(F32),
                                              ALU.subtract)
                    ins.then_inc(keys_lower, 1)

                def lower_queries(c, n):
                    c.act_copied(("q", n))
                    if n >= 2:
                        c.of_turn(q_in[n - 2], 32, 32)
                    elif c.p is not None:
                        c.of_turn(q_in[n - 2 + NCH], 0, 32)
                    cs = slice(n * CH, (n + 1) * CH)
                    for h in range(2):
                        ps = slice(h * DH, (h + 1) * DH)
                        ins = v.tensor_tensor(q_low[ps, n % 2, :], ring[c.ring.use["q", n] % 2][ps, :],
                                              q_s[ps, h, cs].bitcast(F32), ALU.subtract)
                    ins.then_inc(dve_out, 1)

                def scores_out(c, r, c2):
                    c.wait(scored, 2 * r + c2 + 1, 2 * ROWS)
                    if c2 == 0 and r >= PBUF and ("t", former_row(r), 3) in c.ring.use:
                        c.used(("t", former_row(r), 3))
                    if c2 == 1:
                        c.wait(s_out, 2 * r + 1, 2 * ROWS)
                    v.tensor_scalar(probs[:, buffer_of(r), c2 * T // 2:(c2 + 1) * T // 2], s_ps[c2][:],
                                    -SCALE, least[:, r % ROWS, 0:1] if c2 else None, ALU.mult, ALU.min,
                                    accum_out=least[:, r % ROWS, c2:c2 + 1]).then_inc(s_out, 1)

                def transposed_out(c, t, g):
                    c.used(("t", t, g))
                    u = t // 4
                    if u >= 2:
                        c.wait(av_done, u - 1, UNITS)
                    v.tensor_copy(probs_t[:, u % 2, 4 * g:4 * g + 4, t % 2, (t // 2 % 2) * P:(t // 2 % 2 + 1) * P],
                                  ring[c.ring.use["t", t, g] % 2][:].rearrange("p (j n) -> p j n", n=P)
                                  ).then_inc(dve_out, 1)

                def rows_out(c, u):
                    c.wait(exp_out, 4 * u + 4, ROWS)
                    v.tensor_tensor(inv[:], sums[:, 4 * u:4 * u + 4, 0], sums[:, 4 * u:4 * u + 4, 1],
                                    ALU.add).then_inc(dve, 1)
                    c.wait(dve, 2 * u + 1, 2 * UNITS)
                    v.reciprocal(inv[:], inv[:]).then_inc(dve, 1)
                    c.wait(dve, 2 * u + 2, 2 * UNITS)
                    c.used(("o", u))
                    c.wait(gated, u - 1, UNITS, 0, 2)
                    v.tensor_tensor(o_rows[:, u % 2].rearrange("p i h d -> p (i h) d"),
                                    ring[c.ring.use["o", u] % 2][:, 0:2 * P].rearrange("p (n d) -> p n d", d=DH),
                                    inv[:].unsqueeze(2).to_broadcast([P, 4, DH]), ALU.mult
                                    ).then_inc(dve_out, 1)

                def turn(c, ops):
                    for op in ops:
                        if op[0] == "k":
                            lower_keys(c, op[1])
                        elif op[0] == "q":
                            lower_queries(c, op[1])
                        elif op[0] == "t" and copier(*op[1:]) == "dve":
                            transposed_out(c, *op[1:])

                def one_slot(c, slot):
                    t = transposes_in(slot)
                    scores_out(c, slot, 0)
                    if t is not None:
                        transposed_out(c, t, 1)
                    scores_out(c, slot, 1)
                    if t is not None and copier(t, 3) == "dve":
                        transposed_out(c, t, 3)
                    if slot in QUERY_SLOT:
                        lower_queries(c, QUERY_SLOT[slot])
                    if output_in(slot) is not None:
                        rows_out(c, output_in(slot))

                made = [0]

                def link_first(ins):
                    made[0] += 1
                    ins.then_inc(dve_first, 1)
                    eng.wait_ge(dve_first, made[0])

                scratch = probs_t[:].rearrange("p u j h n -> p (u j h n)")[:, 0:2 * XV].rearrange(
                    "p (j e k) -> p j e k", j=2, e=E)
                eng.wait_ge(first_gates, 1)
                c = Counts(eng, AHEAD)
                for i, (what, n) in enumerate(AHEAD_OF_ALL):
                    if i % 2 == 1 and i // 2 < DVE_UNITS:
                        eng.wait_ge(xv_first[i // 2], 16)
                        weigh(v, i // 2, link_first, experts_first(i // 2), v_sb, scratch
                              ).then_inc(first_mixed_dve, 1)
                        eng.wait_ge(first_mixed_dve, i // 2 + 1)
                        if i // 2 == DVE_UNITS - 1:
                            eng.sem_inc(v_in, 8)
                    if what == "k":
                        lower_keys(c, n)
                    else:
                        lower_queries(c, n)
                for slot in FIRST_SLOTS:
                    if slot < PBUF:
                        last_unit = min(UNITS - 1, ((slot + 1) * T - 1) // (2 * XV))
                        eng.wait_ge(first_mixed, last_unit + 1 - DVE_UNITS)
                    one_slot(c, slot)

                with eng.Fori(0, B) as b:
                    eng.wait_ge(used, b * (PAIRS * N_USE + JT) + A_USE)
                    v.memset(acc[:], 0.0).then_inc(acc_zero, 1)
                    with eng.Fori(0, PAIRS) as hp:
                        c = Counts(eng, BODY, b, hp)
                        for slot in OWN_SLOTS:
                            one_slot(c, slot)
                        with eng.If(c.goes_on()):
                            turn(c, TURN)
                            for slot in NEXT_SLOTS:
                                one_slot(c, slot)
                        with eng.If(c.ends()):
                            turn(c, LAST_TURN)
                            c.passed(dve_out, BODY.dve, NO_QUERIES)
                            rows_out(c, UNITS - 2)
                            c.passed(dve_out, BODY.dve, NO_ROWS[0])
                            rows_out(c, UNITS - 1)
                            c.passed(dve_out, BODY.dve, NO_ROWS[1])
                    eng.wait_ge(x1_in, b * 32 + 32)
                    for j in range(JT):
                        eng.wait_ge(projected, b * JT + (j + 1))
                        v.tensor_tensor(last[:, j, :], av[j % 2][:, 0:D], last[:, j, :], ALU.add
                                        ).then_inc(finished, 1)

            @block.tensor
            def _(pe):
                mm = nc.tensor.matmul

                def project(c, n, is_query, bank):
                    c.of_turn(w_in, 32, 32)
                    c.of_turn(x_in[n], 16, 16)
                    for k in range(DC):
                        ins = mm(bank, w_pair[:, k, is_query, :], xc[:, n, k, :], start=(k == 0),
                                 stop=(k == DC - 1))
                    return ins

                def queries(c, n):
                    bank = bank_of(c, ("q", n))
                    project(c, n, 1, bank[:]).then_inc(used, 1)

                def project_keys(c, n):
                    if c.p is not None:
                        c.wait(s_out, 2 * (ROWS - 1) + n // 2 + 1, 2 * ROWS)
                    project(c, n, 0, keys_bank(n)).then_inc(keys, 1)

                def bank_of(c, key):
                    n = c.ring.use[key]
                    if n >= 2:
                        c.copied(c.ring.key[n - 2])
                    elif c.p is None:
                        pass
                    elif n == 0:
                        c.wait(act_out, 0, N_ACT, JT, A_ACT)
                        c.wait(dve_out, -1, N_DVE, 0, A_DVE)
                    else:
                        c.wait(dve_out, 0, N_DVE, 0, A_DVE)
                    return ring[n % 2]

                def scores(c, r, c2):
                    h, i = r % 2, r % ROWS // 2
                    pairs = 1 + r // ROWS
                    if r % 8 == 0 and c2 == 0:
                        c.wait(q_in[r % ROWS // 8], 32 * pairs, 32)
                    if r >= 1:
                        c.wait(s_out, 2 * (r - 1) + c2 + 1, 2 * ROWS)
                    if r % ROWS == 0:
                        c.wait(k_in[c2], 32 * pairs, 32)
                    for n in range(2 * c2, 2 * c2 + 2):
                        to = s_ps[c2][:, (n % 2) * CH:(n % 2 + 1) * CH]
                        q = q_s[:, h, i * P:(i + 1) * P]
                        mm(to, q, k_s[:, 0, h, n * CH:(n + 1) * CH], start=True, stop=False)
                        ins = mm(to, q, k_s[:, 1, h, n * CH:(n + 1) * CH], start=False, stop=True)
                    ins.then_inc(scored, 1)

                def transposes(c, t, g):
                    to = bank_of(c, ("t", t, g))
                    c.wait(exp_out, t + 1, ROWS)
                    for n in range(4):
                        ins = nc.tensor.transpose(to[:, n * P:(n + 1) * P],
                                                  probs[:, buffer_of(t), (4 * g + n) * P:(4 * g + n + 1) * P],
                                                  ident[:])
                    ins.then_inc(used, 1)

                def product(c, u, part, half):
                    if part == 0 and half == 0:
                        if u == 0:
                            c.wait(act_out, 0, N_ACT, JT, A_ACT)
                            c.wait(dve_out, 0, N_DVE, 0, A_DVE)
                            c.wait(v_in, 16, 16)
                        else:
                            c.row_copied(4 * u + 3)
                        if u >= 2:
                            c.wait(av_out, u - 1, UNITS)
                    for j in range(part * AV_STEPS + half * 2, part * AV_STEPS + half * 2 + 2):
                        for h in range(2):
                            ins = mm(av[u % 2][h * DH:(h + 1) * DH, 0:2 * P], v_sb[:, j, h, :],
                                     probs_t[:, u % 2, j, h, :], start=(j == 0), stop=(j == JT - 1))
                    if part == 3 and half == 1:
                        ins.then_inc(av_done, 1)

                def output(c, u):
                    bank = bank_of(c, ("o", u))
                    c.wait(av_out, u + 1, UNITS)
                    for i in range(2):
                        ins = nc.tensor.transpose(bank[:, i * P:(i + 1) * P],
                                                  o_t[:, u % 2, i * P:(i + 1) * P], ident[:])
                    ins.then_inc(used, 1)

                def turn(c, ops):
                    for op in ops:
                        if op[0] == "k":
                            project_keys(c, op[1])
                        elif op[0] == "q":
                            queries(c, op[1])
                        elif op[0] == "t":
                            transposes(c, *op[1:])
                        elif op[0] == "av":
                            product(c, TURN_UNIT, *op[1:])

                def one_slot(c, slot):
                    t = transposes_in(slot)
                    u, part = product_in(slot)
                    scores(c, slot, 0)
                    if t is not None:
                        transposes(c, t, 0)
                    if u is not None:
                        product(c, u, part, 0)
                    if t is not None:
                        transposes(c, t, 1)
                    scores(c, slot, 1)
                    if t is not None:
                        transposes(c, t, 2)
                    if u is not None:
                        product(c, u, part, 1)
                    if t is not None:
                        transposes(c, t, 3)
                    if slot in QUERY_SLOT:
                        queries(c, QUERY_SLOT[slot])
                    if output_in(slot) is not None:
                        output(c, output_in(slot))

                c = Counts(pe, AHEAD)
                for what, n in AHEAD_OF_ALL:
                    if what == "k":
                        project_keys(c, n)
                    else:
                        queries(c, n)
                for slot in FIRST_SLOTS:
                    one_slot(c, slot)
                with pe.Fori(0, B) as b:
                    with pe.Fori(0, PAIRS) as hp:
                        c = Counts(pe, BODY, b, hp)
                        for slot in OWN_SLOTS:
                            one_slot(c, slot)
                        with pe.If(c.goes_on()):
                            turn(c, TURN)
                            for slot in NEXT_SLOTS:
                                one_slot(c, slot)
                        with pe.If(c.ends()):
                            turn(c, LAST_TURN)
                            c.passed(used, BODY.use, NO_QUERIES)
                            product(c, UNITS - 1, 0, 0)
                            output(c, UNITS - 2)
                            for part in range(4):
                                for half in range(2):
                                    if (part, half) != (0, 0):
                                        product(c, UNITS - 1, part, half)
                            c.passed(used, BODY.use, NO_ROWS[0])
                            output(c, UNITS - 1)
                            c.passed(used, BODY.use, NO_ROWS[1])
                    pe.wait_ge(wo_in, 32)
                    pe.wait_ge(dve_out, b * (PAIRS * N_DVE) + (PAIRS * N_DVE + A_DVE))
                    pe.wait_ge(act_out, b * (PAIRS * N_ACT + JT) + (PAIRS * N_ACT + A_ACT))
                    for j in range(JT + 1):
                        if j < JT:
                            pe.wait_ge(gated, b * (PAIRS * UNITS) + ((PAIRS - 1) * UNITS + 2 + j // 2 + 1))
                            if j >= 2:
                                pe.wait_ge(act_out, b * (PAIRS * N_ACT + JT) + (PAIRS * N_ACT + A_ACT + j - 1))
                            a = acc[:, j].rearrange("p e d -> p (e d)")
                            for k in range(3):
                                w = P if k < 2 else DH
                                ins = nc.tensor.transpose(ring[j % 2][0:w, k * P:(k + 1) * P],
                                                          a[:, k * P:k * P + w], ident[:])
                            ins.then_inc(used, 1)
                        if j >= 1:
                            i = j - 1
                            pe.wait_ge(act_out, b * (PAIRS * N_ACT + JT) + (PAIRS * N_ACT + A_ACT + i + 1))
                            if i >= 2:
                                pe.wait_ge(finished, b * JT + (i - 1))
                            for k in range(3):
                                w = P if k < 2 else DH
                                ins = mm(av[i % 2][:, 0:D], acc_t[0:w, i % 2, k, :], wo_sb[0:w, k, :],
                                         start=(k == 0), stop=(k == 2))
                            ins.then_inc(projected, 1)
                    pe.wait_ge(finished, b * JT + JT)

            @block.scalar
            def _(act):
                a = nc.scalar.activation

                def upper_parts(to, n, src):
                    for h in range(2):
                        ps = slice(h * DH, (h + 1) * DH)
                        ins = a(to[ps, h, n * CH:(n + 1) * CH], src[ps, :], ACT.Copy)
                    return ins

                def upper_keys(c, n):
                    c.of_turn(keys, n + 1, NCH)
                    upper_parts(k_s[:, 0], n, keys_bank(n)).then_inc(keys_upper, 1)

                def upper_queries(c, n):
                    c.used(("q", n))
                    upper_parts(q_s, n, ring[c.ring.use["q", n] % 2]).then_inc(act_out, 1)

                def exponentials(c, r, half):
                    if half == 0:
                        c.wait(s_out, 2 * r + 2, 2 * ROWS)
                    x = probs[:, buffer_of(r), half * T // 2:(half + 1) * T // 2]
                    ins = a(x, x, ACT.Exp, bias=least[:, r % ROWS, 1:2], scale=-1.0,
                            accum_out=sums[:, r % ROWS, half:half + 1])
                    if half:
                        ins.then_inc(exp_out, 1)

                def transposed_out(c, t, g):
                    c.used(("t", t, g))
                    u = t // 4
                    if u >= 2:
                        c.wait(av_done, u - 1, UNITS)
                    a(probs_t[:, u % 2, 4 * g:4 * g + 4, t % 2, (t // 2 % 2) * P:(t // 2 % 2 + 1) * P],
                      ring[c.ring.use["t", t, g] % 2][:].rearrange("p (j n) -> p j n", n=P), ACT.Copy
                      ).then_inc(act_out, 1)

                def output_out(c, u):
                    c.wait(av_done, u + 1, UNITS)
                    if u >= 2:
                        c.used(("o", u - 2))
                    a(o_t[:, u % 2, :], av[u % 2][:, 0:2 * P], ACT.Copy).then_inc(av_out, 1)

                def turn(c, ops):
                    for op in ops:
                        if op[0] == "e":
                            exponentials(c, ROWS - 1, op[1])
                        elif op[0] == "k":
                            upper_keys(c, op[1])
                        elif op[0] == "q":
                            upper_queries(c, op[1])
                        elif op[0] == "t" and copier(*op[1:]) == "act":
                            transposed_out(c, *op[1:])

                def one_slot(c, slot):
                    r, t = slot - 1, transposes_in(slot)
                    new_row = slot not in (0, ROWS)
                    if new_row:
                        exponentials(c, r, 0)
                    if t is not None:
                        transposed_out(c, t, 0)
                    if new_row:
                        exponentials(c, r, 1)
                    if output_in(slot) is not None:
                        output_out(c, output_in(slot))
                    if t is not None:
                        transposed_out(c, t, 2)
                        if copier(t, 3) == "act":
                            transposed_out(c, t, 3)
                    if slot in QUERY_SLOT:
                        upper_queries(c, QUERY_SLOT[slot])

                c = Counts(act, AHEAD)
                for what, n in AHEAD_OF_ALL:
                    if what == "k":
                        upper_keys(c, n)
                    else:
                        upper_queries(c, n)
                for slot in FIRST_SLOTS:
                    one_slot(c, slot)
                with act.Fori(0, B) as b:
                    with act.Fori(0, PAIRS) as hp:
                        c = Counts(act, BODY, b, hp)
                        for slot in OWN_SLOTS:
                            one_slot(c, slot)
                        with act.If(c.goes_on()):
                            turn(c, TURN)
                            for slot in NEXT_SLOTS:
                                one_slot(c, slot)
                        with act.If(c.ends()):
                            turn(c, LAST_TURN)
                            c.passed(act_out, BODY.act, NO_QUERIES)
                            output_out(c, UNITS - 2)
                            c.passed(act_out, BODY.act, NO_ROWS[0])
                            output_out(c, UNITS - 1)
                            c.passed(act_out, BODY.act, NO_ROWS[1])
                    for n in (NCH - 2, NCH - 1):
                        act.wait_ge(q_in[n], b * (32 * PAIRS - (32 if n == NCH - 1 else 0)) + 32 * (PAIRS + 1))
                    for j in range(JT):
                        act.wait_ge(used, b * (PAIRS * N_USE + JT) + (PAIRS * N_USE + A_USE + j + 1))
                        if j >= 2:
                            act.wait_ge(projected, b * JT + (j - 1))
                        a(acc_t[:, j % 2, 0:2, :], ring[j % 2][:, 0:2 * P].rearrange("p (c n) -> p c n", c=2), ACT.Copy)
                        a(acc_t[0:DH, j % 2, 2, :], ring[j % 2][0:DH, 2 * P:3 * P], ACT.Copy).then_inc(act_out, 1)


_INS = ["x", "wi_t", "wh_t", "bi", "bh", "wq", "wk", "w_tok", "wo"]


def kernel(L0_attn_x, L0_attn_Wi, L0_attn_bi, L0_attn_Wh, L0_attn_bh, L0_ffn_Wq, L0_ffn_Wk, L0_ffn_Ws,
           L0_ffn_Wd, L0_ffn_Wv, L0_ffn_Wo):
    import numpy as np
    import concourse.bacc as bacc
    from concourse.bass_utils import run_bass_kernel_spmd

    arrays = {
        "x": L0_attn_x,
        "wi_t": np.transpose(L0_attn_Wi),
        "wh_t": np.transpose(L0_attn_Wh),
        "bi": np.transpose(np.reshape(L0_attn_bi, (DC, P))),
        "bh": np.transpose(np.reshape(L0_attn_bh, (DC, P))),
        "wq": L0_ffn_Wq,
        "wk": L0_ffn_Wk,
        "w_tok": np.concatenate([np.reshape(np.transpose(L0_ffn_Wv, (1, 0, 2)), (D, XV)), L0_ffn_Ws, L0_ffn_Wd],
                                axis=1),
        "wo": np.reshape(L0_ffn_Wo, (XV, D)),
    }
    arrays = {k: np.ascontiguousarray(v) for k, v in arrays.items()}
    nc = bacc.Bacc("TRN2", target_bir_lowering=False, num_devices=1, dynamic_dma_scratch_size=1024)
    args = [nc.dram_tensor(k, arrays[k].shape, mybir.dt.from_np(arrays[k].dtype), kind="ExternalInput").ap()
            for k in _INS]
    out = nc.dram_tensor("out", [B, T, D], F32, kind="ExternalOutput").ap()
    build(nc, *args, out)
    r = run_bass_kernel_spmd(nc, [arrays], core_ids=[0])
    return r.results[0]["out"]
```
